# Optimizing a Trainium2 kernel written in Bass

```python
import numpy as np
import jax
import jax.numpy as jnp

def _softmax(x, axis=-1):
    return jax.nn.softmax(x, axis=axis)

def _gelu(x):
    return jax.nn.gelu(x, approximate=True)

def _silu(x):
    return jax.nn.silu(x)

def _sigmoid(x):
    return jax.nn.sigmoid(x)

def _layernorm(x, axis=-1, eps=1e-05):
    m = jnp.mean(x, axis=axis, keepdims=True)
    v = jnp.var(x, axis=axis, keepdims=True)
    return (x - m) / jnp.sqrt(v + eps)

def _scatter_add(tgt, idx, src, axis=0):
    return tgt.at[idx].add(src)

def _segment_sum(src, seg, n):
    return jax.ops.segment_sum(src, seg, n)
kernel_name = 'mk_xattn_ffn_d1_seqx_r8_160c64'

def setup_inputs(seed: int=0):
    np.random.seed(seed)
    _w = jnp.asarray

    def _rec_inputs():
        import jax
        import jax.numpy as jnp
        _rk = jax.random.key(seed)
        x = 7.22e-05 + 1 * jax.random.normal(jax.random.fold_in(_rk, 1), (4, 256, 256), jnp.float32)
        _lenS = 256 - jax.random.randint(jax.random.fold_in(_rk, 7), (4,), 0, max(1, 256 // 4) + 1, jnp.int32)
        _lenS2 = 256 - jax.random.randint(jax.random.fold_in(_rk, 8), (4,), 0, max(1, 256 // 4) + 1, jnp.int32)
        _ctx_1024P = jax.random.normal(jax.random.fold_in(_rk, 11), (4, 16, 128), jnp.float32)
        _ctx_1024c = jax.random.dirichlet(jax.random.fold_in(_rk, 511), 0.3 * jnp.ones((16,), jnp.float32), (4, 256))
        _ctx_1024t = jnp.einsum('bsk,bkd->bsd', _ctx_1024c, _ctx_1024P)
        _ctx_1024t = _ctx_1024t * jax.lax.rsqrt(jnp.mean(jnp.square(_ctx_1024t)) + 1e-12) * 0.953939
        ctx_1024 = 2.81802e-05 + 1.00001 * (_ctx_1024t + 0.3 * jax.random.normal(jax.random.fold_in(_rk, 611), (4, 256, 128), jnp.float32))
        return (x, ctx_1024)
    x, ctx_1024 = _rec_inputs()

    def _L0_xattn_setup():
        import jax, jax.numpy as jnp
        import numpy as np
        key = jax.random.key(seed)
        ks = jax.random.split(key, 6)
        B, L, N, C, D = (8, 64, 256, 128, 128)
        return {'teacher_logits': jax.random.normal(ks[0], (B, L, N), dtype=jnp.float32), 'teacher_features': jax.random.normal(ks[1], (B, N, C), dtype=jnp.float32), 'Wq': jax.random.normal(ks[2], (D, C), dtype=jnp.float32) * (1.0 / np.sqrt(C)), 'bq': jnp.zeros((D,), dtype=jnp.float32), 'Wk': jax.random.normal(ks[3], (D, C), dtype=jnp.float32) * (1.0 / np.sqrt(C)), 'bk': jnp.zeros((D,), dtype=jnp.float32)}
    _L0_xattn_all = _L0_xattn_setup()
    _L0_xattn_in = {k: v for k, v in _L0_xattn_all.items() if k in ('Wq', 'bq', 'Wk', 'bk')}
    del _L0_xattn_all

    def _L0_ffn_setup():
        import jax, jax.numpy as jnp
        import numpy as np
        N_EXPERTS = 8
        TOP_K = 2
        C = 256
        H = 128
        HS = 256
        B, T = (1, 64)
        SCALE = 0.02
        key = jax.random.key(seed)
        ks = jax.random.split(key, 10)
        x = jax.random.normal(ks[0], (B, T, C), dtype=jnp.float32)
        gate_w = jax.random.normal(ks[1], (N_EXPERTS, C), dtype=jnp.float32) * SCALE
        w_gate = jax.random.normal(ks[2], (N_EXPERTS, H, C), dtype=jnp.float32) * SCALE
        w_up = jax.random.normal(ks[3], (N_EXPERTS, H, C), dtype=jnp.float32) * SCALE
        w_down = jax.random.normal(ks[4], (N_EXPERTS, C, H), dtype=jnp.float32) * SCALE
        sh_gate = jax.random.normal(ks[5], (HS, C), dtype=jnp.float32) * SCALE
        sh_up = jax.random.normal(ks[6], (HS, C), dtype=jnp.float32) * SCALE
        sh_down = jax.random.normal(ks[7], (C, HS), dtype=jnp.float32) * SCALE
        se_gate_w = jax.random.normal(ks[8], (1, C), dtype=jnp.float32) * SCALE
        return {'x': x, 'gate_w': gate_w, 'w_gate': w_gate, 'w_up': w_up, 'w_down': w_down, 'sh_gate': sh_gate, 'sh_up': sh_up, 'sh_down': sh_down, 'se_gate_w': se_gate_w}
    _L0_ffn_all = _L0_ffn_setup()
    _L0_ffn_in = {k: v for k, v in _L0_ffn_all.items() if k in ('gate_w', 'w_gate', 'w_up', 'w_down', 'sh_gate', 'sh_up', 'sh_down', 'se_gate_w')}
    del _L0_ffn_all
    return {'x': x, 'ctx_1024': ctx_1024, 'L0_xattn_Wq': _L0_xattn_in['Wq'], 'L0_xattn_bq': _L0_xattn_in['bq'], 'L0_xattn_Wk': _L0_xattn_in['Wk'], 'L0_xattn_bk': _L0_xattn_in['bk'], 'L0_ffn_gate_w': _L0_ffn_in['gate_w'], 'L0_ffn_w_gate': _L0_ffn_in['w_gate'], 'L0_ffn_w_up': _L0_ffn_in['w_up'], 'L0_ffn_w_down': _L0_ffn_in['w_down'], 'L0_ffn_sh_gate': _L0_ffn_in['sh_gate'], 'L0_ffn_sh_up': _L0_ffn_in['sh_up'], 'L0_ffn_sh_down': _L0_ffn_in['sh_down'], 'L0_ffn_se_gate_w': _L0_ffn_in['se_gate_w']}

def reference(x, ctx_1024, L0_xattn_Wq, L0_xattn_bq, L0_xattn_Wk, L0_xattn_bk, L0_ffn_gate_w, L0_ffn_w_gate, L0_ffn_w_up, L0_ffn_w_down, L0_ffn_sh_gate, L0_ffn_sh_up, L0_ffn_sh_down, L0_ffn_se_gate_w):
    import jax
    import jax.numpy as jnp

    def _L0_xattn_ref(teacher_logits, teacher_features, Wq, bq, Wk, bk):
        import jax, jax.numpy as jnp
        import numpy as np
        query = jnp.einsum('bnc,dc->bnd', teacher_features, Wq) + bq
        key = jnp.einsum('bnc,dc->bnd', teacher_features, Wk) + bk
        energy = jnp.einsum('bnd,bmd->bnm', query, key)
        attention = jax.nn.softmax(energy, axis=-1)
        x_m = jnp.einsum('bln,bmn->blm', teacher_logits, attention)
        return x_m

    def _L0_ffn_ref(x, gate_w, w_gate, w_up, w_down, sh_gate, sh_up, sh_down, se_gate_w):
        import jax, jax.numpy as jnp
        import numpy as np
        N_EXPERTS = 8
        TOP_K = 2
        C = 256
        H = 128
        HS = 256
        B, T = (1, 64)
        SCALE = 0.02
        Bb, Tt, Cc = x.shape
        xf = x.reshape(-1, Cc)
        scores = xf @ gate_w.T
        ew, ei = jax.lax.top_k(scores, TOP_K)
        ew = jax.nn.softmax(ew, axis=-1)
        x1 = jax.nn.silu(jnp.einsum('td,ehd->teh', xf, w_gate))
        x3 = jnp.einsum('td,ehd->teh', xf, w_up)
        expert_out = jnp.einsum('teh,edh->ted', x1 * x3, w_down)
        onehot = jax.nn.one_hot(ei, N_EXPERTS, dtype=ew.dtype)
        comb = jnp.einsum('ta,tae->te', ew, onehot)
        routed = jnp.einsum('te,ted->td', comb, expert_out)
        shared = jax.nn.silu(xf @ sh_gate.T) * (xf @ sh_up.T) @ sh_down.T
        sgate = jax.nn.sigmoid(xf @ se_gate_w.T)
        return (routed + sgate * shared).reshape(Bb, Tt, Cc)
    x = x + _L0_xattn_ref(_layernorm(x, axis=-1), ctx_1024, L0_xattn_Wq, L0_xattn_bq, L0_xattn_Wk, L0_xattn_bk)
    x = x + _L0_ffn_ref(_layernorm(x, axis=-1), L0_ffn_gate_w, L0_ffn_w_gate, L0_ffn_w_up, L0_ffn_w_down, L0_ffn_sh_gate, L0_ffn_sh_up, L0_ffn_sh_down, L0_ffn_se_gate_w)
    return x

_drawn_inputs = setup_inputs


def setup_inputs(seed=0):
    import zlib

    import numpy as np

    out = dict(_drawn_inputs(seed))
    spreads = {'L0_xattn_bq': (0.0, 0.1), 'L0_xattn_bk': (0.0, 0.8)}
    factors = {'L0_ffn_gate_w': 8.0,
     'L0_ffn_w_gate': 8.0,
     'L0_ffn_w_up': 8.0,
     'L0_ffn_w_down': 8.0,
     'L0_ffn_sh_gate': 8.0,
     'L0_ffn_sh_up': 8.0,
     'L0_ffn_sh_down': 8.0,
     'L0_ffn_se_gate_w': 8.0}
    for name, (base, spread) in spreads.items():
        noise = np.random.default_rng([zlib.crc32(name.encode()), seed]).standard_normal(out[name].shape)
        drawn = base * np.exp(spread * noise) if base else spread * noise
        out[name] = jnp.asarray(drawn.astype(out[name].dtype))
    for name, factor in factors.items():
        out[name] = (out[name] * factor).astype(out[name].dtype)
    return out
```

```python
from contextlib import ExitStack

import numpy as np
import concourse.bass as bass
from concourse import mybir

P = 128
B = 4
L = 256
D = 128
E = 8
LT = L // P
KT = L // P
HB = 2
HT = HB * LT
N = HB * L
UNITS = E + 2
R = E + 2
WU = 3 * KT * P
EPS = 1e-5
RSQRT_SEED = float(0x5F3759DF)

F32 = mybir.dt.float32
F32R = mybir.dt.float32r
I32 = mybir.dt.int32
U32 = mybir.dt.uint32
ALU = mybir.AluOpType
ACT = mybir.ActivationFunctionType
AX = mybir.AxisListType


def xattn_moe_kernel(nc, proj, x, router, ffn, out):
    with ExitStack() as ctx:
        def sb(name, shape, dt=F32):
            return ctx.enter_context(nc.sbuf_tensor(name, shape, dt))

        def sem(name):
            return ctx.enter_context(nc.semaphore(name))

        bank = [ctx.enter_context(nc.psum_tensor(f"bank{i}", [P, 512], F32)) for i in range(8)]
        gate_ps, up_ps, comb_ps = bank[0], bank[1], bank[2]
        acc_ps = bank[3:5]

        proj_sb = sb("proj_sb", [P, 2 + 2 * D + B * L])
        x_sb = sb("x_sb", [P, B * LT, L])
        router_sb = sb("router_sb", [P, KT, R])
        router_hi = sb("router_hi", [P, KT, R], F32R)
        router_lo = sb("router_lo", [P, KT, R], F32R)
        ffn_sb = sb("ffn_sb", [P, UNITS, WU])
        ffn_hi = sb("ffn_hi", [P, UNITS, WU], F32R)
        ffn_lo = sb("ffn_lo", [P, UNITS, WU], F32R)
        ident = sb("ident", [P, P])
        zeros = sb("zeros", [P, P])
        iota8 = sb("iota8", [P, HT, E])
        qT = sb("qT", [P, B * L])
        kT = sb("kT", [P, B * L])
        stats = sb("stats", [P, B * LT, 6])
        mv = sb("mv", [P, B * LT, 2])
        veps = sb("veps", [P, B * LT])
        seed = sb("seed", [P, B * LT], I32)
        yy = sb("yy", [P, B * LT])
        rstd = sb("rstd", [P, B * LT])
        xln = sb("xln", [P, B * LT, L])
        xlnT = sb("xlnT", [P, B, KT, L])
        nmax = sb("nmax", [P, B * LT])
        psums = sb("psums", [P, B * LT])
        rsum = sb("rsum", [P, B * LT])
        pexp = sb("pexp", [P, B, LT, L])
        probT = sb("probT", [P, B, KT, L])
        x1 = sb("x1", [P, B * LT, L])
        stats2 = sb("stats2", [P, B * LT, 6])
        mv2 = sb("mv2", [P, B * LT, 2])
        rstd2 = sb("rstd2", [P, B * LT])
        xn = xln
        x1T = sb("x1T", [P, KT, B * L])
        xnT_hi = sb("xnT_hi", [P, KT, B * L], F32R)
        xnT_lo = sb("xnT_lo", [P, KT, B * L], F32R)
        score = sb("score", [P, HT, R])
        top = sb("top", [P, HT, 8])
        topi = sb("topi", [P, HT, 8], U32)
        topf = sb("topf", [P, HT, 2])
        rarg = sb("rarg", [P, HT, 2])
        rexp = sb("rexp", [P, 2, HT, 2])
        rden = sb("rden", [P, HT, 2])
        rinv = sb("rinv", [P, HT, 2])
        pick0 = sb("pick0", [P, HT, E])
        pick1 = sb("pick1", [P, HT, E])
        comb = sb("comb", [P, 2, HT, E + 1])
        silu_sb = sb("silu_sb", [P, N])
        weighted = sb("weighted", [P, N])
        act_sb = sb("act_sb", [P, N])
        act_hi = sb("act_hi", [P, 2, N], F32R)
        act_lo = sb("act_lo", [P, 2, N], F32R)
        out_sb = sb("out_sb", [P, 2, KT, N])

        proj_in = [sem("proj_in0"), sem("proj_in1")]
        x_in = [sem("x_in0"), sem("x_in1")]
        router_in = sem("router_in")
        ffn_in = [sem(f"ffn_in{u}") for u in range(UNITS)]
        const_ready = sem("const_ready")
        pool_step = sem("pool_step")
        router_split = sem("router_split")
        ffn_split = sem("ffn_split")
        qk_ready, qk_stored = sem("qk_ready"), sem("qk_stored")
        xln_ready, xlnT_ready, xlnT_stored = sem("xln_ready"), sem("xlnT_ready"), sem("xlnT_stored")
        energy_ready, nmax_ready, exp_ready = sem("energy_ready"), sem("nmax_ready"), sem("exp_ready")
        prob_ready, probT_ready, probT_stored = sem("prob_ready"), sem("probT_ready"), sem("probT_stored")
        xm_ready, x1_ready, xn_ready = sem("xm_ready"), sem("x1_ready"), sem("xn_ready")
        xnT_ready, xnT_hi_ready, xnT_lo_ready = sem("xnT_ready"), sem("xnT_hi_ready"), sem("xnT_lo_ready")
        x1T_ready, x1T_stored = sem("x1T_ready"), sem("x1T_stored")
        score_ready, rarg_ready, rexp_ready = sem("score_ready"), sem("rarg_ready"), sem("rexp_ready")
        comb_ready = sem("comb_ready")
        cb_ready, gate_ready, up_ready, down_ready = (sem("cb_ready"), sem("gate_ready"), sem("up_ready"),
                                                      sem("down_ready"))
        silu_ready, weighted_ready, act_ready = sem("silu_ready"), sem("weighted_ready"), sem("act_ready")
        act_hi_ready, act_lo_ready = sem("act_hi_ready"), sem("act_lo_ready")
        out_ready, out_stored = sem("out_ready"), sem("out_stored")
        dve_step = sem("dve_step")

        bq, bk = proj_sb[:, 0:1], proj_sb[:, 1:2]
        wqT, wkT = proj_sb[:, 2:2 + D], proj_sb[:, 2 + D:2 + 2 * D]
        C0 = 2 + 2 * D
        ctxT = proj_sb[:, C0:C0 + B * L]

        E_BANK = [bank[6], bank[1], bank[5], bank[6]]
        XLNT_BANK = [bank[5], bank[0], bank[3], bank[4]]
        PT_BANK = [bank[7], bank[2], bank[7], bank[5]]
        XM_BANK = [bank[5], bank[0], bank[6], bank[7]]
        XNT_BANK = [bank[6], bank[1], bank[5], bank[6]]
        X1T_BANK = [bank[7], bank[2], bank[7], bank[5]]
        SCORE_BANK = [bank[5], bank[6]]

        def tiles(ps):
            return ps[:, :].rearrange("p (t n) -> p t n", t=2)

        def scores_of(h):
            return SCORE_BANK[h][:, 0:HT * R].rearrange("p (t r) -> p t r", t=HT)

        def w_of(w, g, kind, k):
            c = (kind * KT + k) * P
            return w[:, g % UNITS, c:c + P]

        block = ctx.enter_context(nc.Block())

        @block.sync
        def _(sp):
            sp.dma_start(proj_sb[:, 0:C0 + N], proj[:, 0:C0 + N]).then_inc(proj_in[0], 16)
            sp.dma_start(proj_sb[:, C0 + N:], proj[:, C0 + N:]).then_inc(proj_in[1], 16)
            sp.dma_start(router_sb[:], router).then_inc(router_in, 16)
            for u in range(UNITS):
                sp.dma_start(ffn_sb[:, u, :], ffn[u]).then_inc(ffn_in[u], 16)
            for h in range(2):
                for k in range(KT):
                    sp.wait_ge(out_ready, h * KT + k + 1)
                    sp.dma_start(out[k, :, h * N:(h + 1) * N], out_sb[:, h, k, :]).then_inc(out_stored, 16)
            sp.wait_ge(out_stored, 16 * 2 * KT)

        @block.gpsimd
        def _(pool):
            pool.memset(zeros[:], 0.0).then_inc(pool_step, 1)
            pool.wait_ge(pool_step, 1)
            pool.affine_select(out=ident[:], in_=zeros[:], compare_op=ALU.not_equal, fill=1.0, base=0,
                               pattern=[[-1, P]], channel_multiplier=1)
            pool.iota(iota8[:], pattern=[[0, HT], [1, E]], base=0, channel_multiplier=0,
                      allow_small_or_imprecise_dtypes=True).then_inc(const_ready, 1)
            pool.wait_ge(router_in, 16)
            pool.tensor_copy(router_hi[:], router_sb[:]).then_inc(pool_step, 1)
            pool.wait_ge(pool_step, 2)
            pool.tensor_tensor(router_lo[:], router_sb[:], router_hi[:].bitcast(F32),
                               ALU.subtract).then_inc(router_split, 1)
            for u in range(UNITS):
                pool.wait_ge(ffn_in[u], 16)
                pool.tensor_copy(ffn_hi[:, u, :], ffn_sb[:, u, :]).then_inc(pool_step, 1)
                pool.wait_ge(pool_step, u + 3)
                pool.tensor_tensor(ffn_lo[:, u, :], ffn_sb[:, u, :], ffn_hi[:, u, :].bitcast(F32),
                                   ALU.subtract).then_inc(ffn_split, 1)

        @block.scalar
        def _(act):
            for h in range(2):
                act.dma_start(x_sb[:, h * HT:(h + 1) * HT, :],
                              x[h * HT:(h + 1) * HT].rearrange("t p n -> p t n")).then_inc(x_in[h], 16)

            def store_qk(h):
                for i, (dst, bias) in enumerate(((qT, bq), (kT, bk))):
                    act.wait_ge(qk_ready, 2 * h + i + 1)
                    act.activation(dst[:, h * N:(h + 1) * N], acc_ps[i][:, :], ACT.Identity,
                                   bias=bias).then_inc(qk_stored, 1)

            def store_xlnT(b):
                act.wait_ge(xlnT_ready, b + 1)
                act.copy(xlnT[:, b], tiles(XLNT_BANK[b])).then_inc(xlnT_stored, 1)

            def exps(b):
                act.wait_ge(nmax_ready, b + 1)
                for t in range(LT):
                    i = b * LT + t
                    last = act.activation(pexp[:, b, t, :], tiles(E_BANK[b])[:, t, :], ACT.Exp,
                                          bias=nmax[:, i:i + 1], accum_out=psums[:, i:i + 1])
                last.then_inc(exp_ready, 1)

            def store_probT(b):
                act.wait_ge(probT_ready, b + 1)
                act.copy(probT[:, b], tiles(PT_BANK[b])).then_inc(probT_stored, 1)

            def store_xnT_hi(b):
                act.wait_ge(xnT_ready, b + 1)
                act.copy(xnT_hi[:, :, b * L:(b + 1) * L], tiles(XNT_BANK[b])).then_inc(xnT_hi_ready, 1)

            def store_x1T(b):
                act.wait_ge(x1T_ready, b + 1)
                act.copy(x1T[:, :, b * L:(b + 1) * L], tiles(X1T_BANK[b])).then_inc(x1T_stored, 1)

            def routing_exp(h):
                act.wait_ge(rarg_ready, h + 1)
                act.activation(rexp[:, h], rarg[:], ACT.Exp).then_inc(rexp_ready, 1)

            store_qk(0)
            for b in range(HB):
                exps(b)
                store_xlnT(b)
            store_qk(1)
            for b in range(HB):
                store_probT(b)
            for b in range(HB, B):
                store_xlnT(b)
            for b in range(HB):
                store_xnT_hi(b)
            for b in range(HB):
                store_x1T(b)
            routing_exp(0)
            between = {0: [(exps, 2), (exps, 3)], 2: [(store_probT, 2), (store_probT, 3)],
                       6: [(store_xnT_hi, 2), (store_xnT_hi, 3), (store_x1T, 2)], 7: [(store_x1T, 3)],
                       8: [(routing_exp, 1)]}
            for g in range(2 * UNITS):
                act.wait_ge(gate_ready, g + 1)
                if g >= 1:
                    act.wait_ge(weighted_ready, g)
                act.activation(silu_sb[:], gate_ps[:, :], ACT.Silu).then_inc(silu_ready, 1)
                act.wait_ge(act_ready, g + 1)
                if g >= 2:
                    act.wait_ge(down_ready, g - 1)
                act.copy(act_hi[:, g % 2, :], act_sb[:]).then_inc(act_hi_ready, 1)
                for step, i in between.get(g, []):
                    step(i)

        @block.vector
        def _(dve):
            count = [0]

            def then(ins):
                count[0] += 1
                ins.then_inc(dve_step, 1)
                dve.wait_ge(dve_step, count[0])

            def rsqrt(y, var, n0, n1):
                v, s, t = veps[:, n0:n1], seed[:, n0:n1], yy[:, n0:n1]
                then(dve.tensor_scalar(v, var, EPS, None, ALU.add))
                then(dve.tensor_scalar(s, v.bitcast(I32), 1, None, ALU.logical_shift_right))
                then(dve.tensor_scalar(y.bitcast(I32), s, -1.0, RSQRT_SEED, ALU.mult, ALU.add))
                for _ in range(3):
                    then(dve.scalar_tensor_tensor(t, y, -0.5, y, ALU.mult, ALU.mult))
                    then(dve.tensor_tensor(t, t, v, ALU.mult))
                    then(dve.scalar_tensor_tensor(y, t, 1.5, y, ALU.add, ALU.mult))

            def moments(src, st, m, i):
                dve.bn_stats(st[:, i, :], src[:, i, :])

            def norm1_stats(h):
                dve.wait_ge(x_in[h], 16)
                for i in range(h * HT, (h + 1) * HT):
                    last = dve.bn_stats(stats[:, i, :], x_sb[:, i, :])
                then(last)
                for i in range(h * HT, (h + 1) * HT):
                    last = dve.bn_aggr(mv[:, i, :], stats[:, i, :])
                then(last)
                rsqrt(rstd[:, h * HT:(h + 1) * HT], mv[:, h * HT:(h + 1) * HT, 1], h * HT, (h + 1) * HT)

            def norm1(b):
                for i in range(b * LT, (b + 1) * LT):
                    last = dve.tensor_scalar(xln[:, i, :], x_sb[:, i, :], mv[:, i, 0:1], rstd[:, i:i + 1],
                                             ALU.subtract, ALU.mult)
                last.then_inc(xln_ready, 1)

            def row_max(b):
                dve.wait_ge(energy_ready, b + 1)
                dve.reduce_max(nmax[:, b * LT:(b + 1) * LT], tiles(E_BANK[b]), AX.X,
                               negate=True).then_inc(nmax_ready, 1)

            def normalise(b):
                dve.wait_ge(exp_ready, b + 1)
                then(dve.reciprocal(rsum[:, b * LT:(b + 1) * LT], psums[:, b * LT:(b + 1) * LT]))
                for t in range(LT):
                    i = b * LT + t
                    last = dve.tensor_scalar(pexp[:, b, t, :], pexp[:, b, t, :], rsum[:, i:i + 1], None, ALU.mult)
                last.then_inc(prob_ready, 1)

            def add_attention(b):
                dve.wait_ge(xm_ready, b + 1)
                dve.tensor_tensor(x1[:, b * LT:(b + 1) * LT, :], tiles(XM_BANK[b]),
                                  x_sb[:, b * LT:(b + 1) * LT, :], ALU.add).then_inc(x1_ready, 1)

            def norm2_stats(b):
                dve.wait_ge(x1_ready, b + 1)
                for i in range(b * LT, (b + 1) * LT):
                    last = dve.bn_stats(stats2[:, i, :], x1[:, i, :])
                then(last)
                for i in range(b * LT, (b + 1) * LT):
                    last = dve.bn_aggr(mv2[:, i, :], stats2[:, i, :])
                then(last)

            def norm2(h):
                n0, n1 = h * HT, (h + 1) * HT
                rsqrt(rstd2[:, n0:n1], mv2[:, n0:n1, 1], n0, n1)
                for i in range(n0, n1):
                    last = dve.tensor_scalar(xn[:, i, :], x1[:, i, :], mv2[:, i, 0:1], rstd2[:, i:i + 1],
                                             ALU.subtract, ALU.mult)
                    if i % LT == LT - 1:
                        last.then_inc(xn_ready, 1)

            def store_xnT_lo(b):
                dve.wait_ge(xnT_hi_ready, b + 1)
                cols = slice(b * L, (b + 1) * L)
                dve.tensor_tensor(xnT_lo[:, :, cols], tiles(XNT_BANK[b]), xnT_hi[:, :, cols].bitcast(F32),
                                  ALU.subtract).then_inc(xnT_lo_ready, 1)

            def top_two(h):
                dve.wait_ge(score_ready, h + 1)
                then(dve.tensor_copy(score[:], scores_of(h)))
                for t in range(HT):
                    last = dve.max(top[:, t, :], score[:, t, 0:E])
                then(last)
                for t in range(HT):
                    dve.max_index(topi[:, t, :], top[:, t, :], score[:, t, 0:E])
                dve.tensor_tensor(rarg[:, :, 0], top[:, :, 1], top[:, :, 0], ALU.subtract)
                dve.tensor_scalar(rarg[:, :, 1], score[:, :, E], -1.0, None, ALU.mult).then_inc(rarg_ready, 1)

            def combine(h):
                dve.wait_ge(rexp_ready, h + 1)
                dve.tensor_copy(topf[:], topi[:, :, 0:2])
                then(dve.tensor_scalar(rden[:], rexp[:, h], 1.0, None, ALU.add))
                then(dve.reciprocal(rinv[:], rden[:]))
                then(dve.tensor_tensor(rden[:, :, 1], rinv[:, :, 0], rexp[:, h, :, 0], ALU.mult))
                for t in range(HT):
                    dve.tensor_scalar(pick0[:, t, :], iota8[:, t, :], topf[:, t, 0:1], rinv[:, t, 0:1],
                                      ALU.is_equal, ALU.mult)
                    last = dve.tensor_scalar(pick1[:, t, :], iota8[:, t, :], topf[:, t, 1:2], rden[:, t, 1:2],
                                             ALU.is_equal, ALU.mult)
                then(last)
                dve.tensor_copy(comb[:, h, :, E], rinv[:, :, 1])
                dve.tensor_tensor(comb[:, h, :, 0:E], pick0[:], pick1[:], ALU.add).then_inc(comb_ready, 1)

            def finish(h):
                dve.wait_ge(down_ready, (h + 1) * UNITS)
                dve.wait_ge(x1T_stored, (h + 1) * HB)
                for k in range(KT):
                    dve.tensor_tensor(out_sb[:, h, k, :], acc_ps[k][:, :], x1T[:, k, h * N:(h + 1) * N],
                                      ALU.add).then_inc(out_ready, 1)

            dve.wait_ge(const_ready, 1)
            norm1_stats(0)
            row_max(0)
            row_max(1)
            norm1(0)
            norm1(1)
            normalise(0)
            normalise(1)
            norm1_stats(1)
            norm1(2)
            norm1(3)
            for b in range(HB):
                add_attention(b)
                norm2_stats(b)
            norm2(0)
            for b in range(HB):
                store_xnT_lo(b)
            top_two(0)
            combine(0)
            between = {0: [(row_max, 2), (row_max, 3)], 1: [(normalise, 2), (normalise, 3)],
                       3: [(add_attention, 2), (add_attention, 3)], 4: [(norm2_stats, 2), (norm2_stats, 3)],
                       5: [(norm2, 1)], 6: [(store_xnT_lo, 2), (store_xnT_lo, 3)],
                       7: [(top_two, 1)], 8: [(combine, 1)], UNITS: [(finish, 0)]}
            for g in range(2 * UNITS):
                dve.wait_ge(silu_ready, g + 1)
                dve.wait_ge(cb_ready, g + 1)
                dve.tensor_tensor(weighted[:], comb_ps[:, :], silu_sb[:], ALU.mult).then_inc(weighted_ready, 1)
                dve.wait_ge(weighted_ready, g + 1)
                dve.wait_ge(up_ready, g + 1)
                dve.tensor_tensor(act_sb[:], up_ps[:, :], weighted[:], ALU.mult).then_inc(act_ready, 1)
                dve.wait_ge(act_hi_ready, g + 1)
                dve.tensor_tensor(act_lo[:, g % 2, :], act_sb[:], act_hi[:, g % 2, :].bitcast(F32),
                                  ALU.subtract).then_inc(act_lo_ready, 1)
                for step, i in between.get(g, []):
                    step(i)
            finish(1)

        @block.tensor
        def _(pe):
            def project(h):
                for i, w in enumerate((wqT, wkT)):
                    if h:
                        pe.wait_ge(qk_stored, i + 1)
                    pe.matmul(acc_ps[i][:, :], w, ctxT[:, h * N:(h + 1) * N], start=True,
                              stop=True).then_inc(qk_ready, 1)

            def transpose4(dst, src):
                for k in range(KT):
                    for t in range(LT):
                        last = pe.transpose(dst[:, k, t * P:(t + 1) * P], src[:, t, k * P:(k + 1) * P], ident[:])
                return last

            def energy(b):
                pe.wait_ge(qk_stored, 2 * (b // HB) + 2)
                for t in range(LT):
                    n = b * L + t * P
                    last = pe.matmul(tiles(E_BANK[b])[:, t, :], qT[:, n:n + P], kT[:, b * L:(b + 1) * L],
                                     start=True, stop=True)
                last.then_inc(energy_ready, 1)

            def transpose_xln(b):
                pe.wait_ge(xln_ready, b + 1)
                transpose4(tiles(XLNT_BANK[b]), xln[:, b * LT:(b + 1) * LT, :]).then_inc(xlnT_ready, 1)

            def transpose_prob(b):
                pe.wait_ge(prob_ready, b + 1)
                transpose4(tiles(PT_BANK[b]), pexp[:, b]).then_inc(probT_ready, 1)

            def attend(b):
                pe.wait_ge(xlnT_stored, b + 1)
                pe.wait_ge(probT_stored, b + 1)
                for t in range(LT):
                    for k in range(KT):
                        last = pe.matmul(tiles(XM_BANK[b])[:, t, :], xlnT[:, b, k, t * P:(t + 1) * P],
                                         probT[:, b, k, :], start=(k == 0), stop=(k == KT - 1))
                last.then_inc(xm_ready, 1)

            def transpose_xn(b):
                pe.wait_ge(xn_ready, b + 1)
                transpose4(tiles(XNT_BANK[b]), xn[:, b * LT:(b + 1) * LT, :]).then_inc(xnT_ready, 1)

            def transpose_x1(b):
                transpose4(tiles(X1T_BANK[b]), x1[:, b * LT:(b + 1) * LT, :]).then_inc(x1T_ready, 1)

            def route(h):
                pe.wait_ge(router_split, 1)
                pe.wait_ge(xnT_lo_ready, (h + 1) * HB)
                for t in range(HT):
                    cols = slice(h * N + t * P, h * N + (t + 1) * P)
                    parts = [(a, w, k) for k in range(KT) for a in (xnT_lo, xnT_hi)
                             for w in (router_lo, router_hi)]
                    for i, (a, w, k) in enumerate(parts):
                        last = pe.matmul(scores_of(h)[:, t, :], a[:, k, cols], w[:, k, :],
                                         start=(i == 0), stop=(i == len(parts) - 1))
                last.then_inc(score_ready, 1)

            def weights_of_tokens(g):
                h, e = g // UNITS, min(g % UNITS, E)
                pe.wait_ge(comb_ready, h + 1)
                if g >= 1:
                    pe.wait_ge(weighted_ready, g)
                for t in range(HT):
                    last = pe.transpose(comb_ps[:, t * P:(t + 1) * P],
                                        comb[:, h, t, e:e + 1].broadcast_to([P, P]), ident[:])
                last.then_inc(cb_ready, 1)

            def hidden(g, kind, ps):
                cols = slice(g // UNITS * N, (g // UNITS + 1) * N)
                parts = [(w, a, k) for k in range(KT) for w, a in
                         ((ffn_hi, xnT_hi), (ffn_hi, xnT_lo), (ffn_lo, xnT_hi))]
                for i, (w, a, k) in enumerate(parts):
                    last = pe.matmul(ps[:, :], w_of(w, g, kind, k), a[:, k, cols],
                                     start=(i == 0), stop=(i == len(parts) - 1))
                return last

            def down(g):
                if g == UNITS:
                    pe.wait_ge(out_ready, KT)
                for parts, ready in ((((ffn_hi, act_hi), (ffn_lo, act_hi)), act_hi_ready),
                                     (((ffn_hi, act_lo),), act_lo_ready)):
                    pe.wait_ge(ready, g + 1)
                    for k in range(KT):
                        for w, a in parts:
                            last = pe.matmul(acc_ps[k][:, :], w_of(w, g, 2, k), a[:, g % 2, :],
                                             start=(g % UNITS == 0 and w is ffn_hi and a is act_hi),
                                             stop=(g % UNITS == UNITS - 1 and a is act_lo))
                last.then_inc(down_ready, 1)

            pe.wait_ge(proj_in[0], 16)
            project(0)
            for b in range(HB):
                energy(b)
            pe.wait_ge(const_ready, 1)
            for b in range(HB):
                transpose_xln(b)
            pe.wait_ge(proj_in[1], 16)
            project(1)
            for b in range(HB):
                transpose_prob(b)
            for b in range(HB):
                attend(b)
            pe.wait_ge(qk_stored, 4)
            for b in range(HB, B):
                transpose_xln(b)
            for b in range(HB):
                transpose_xn(b)
            for b in range(HB):
                transpose_x1(b)
            route(0)

            def before_second(step):
                if step is energy:
                    pe.wait_ge(rarg_ready, 1)
                    pe.wait_ge(xnT_lo_ready, HB)
                    pe.wait_ge(x1T_stored, HB)
                elif step is transpose_prob:
                    pe.wait_ge(exp_ready, 3)
                elif step is attend:
                    pe.wait_ge(exp_ready, 4)
                    pe.wait_ge(probT_stored, 4)
                elif step is transpose_xn:
                    pe.wait_ge(x1_ready, 4)
                elif step is transpose_x1:
                    pe.wait_ge(xnT_lo_ready, 3)

            between = {0: [(energy, 2), (energy, 3)], 2: [(transpose_prob, 2), (transpose_prob, 3)],
                       3: [(attend, 2), (attend, 3)],
                       6: [(transpose_xn, 2), (transpose_xn, 3)],
                       7: [(transpose_x1, 2), (transpose_x1, 3), (route, 1)]}
            for g in range(2 * UNITS):
                weights_of_tokens(g)
                if g < UNITS:
                    pe.wait_ge(ffn_split, g + 1)
                if g >= 1:
                    pe.wait_ge(silu_ready, g)
                hidden(g, 0, gate_ps).then_inc(gate_ready, 1)
                if g >= 1:
                    pe.wait_ge(act_ready, g)
                hidden(g, 1, up_ps).then_inc(up_ready, 1)
                for step, i in between.get(g, []):
                    before_second(step)
                    step(i)
                if g >= 1:
                    down(g - 1)
            down(2 * UNITS - 1)


def kernel(x, ctx_1024, L0_xattn_Wq, L0_xattn_bq, L0_xattn_Wk, L0_xattn_bk, L0_ffn_gate_w, L0_ffn_w_gate,
           L0_ffn_w_up, L0_ffn_w_down, L0_ffn_sh_gate, L0_ffn_sh_up, L0_ffn_sh_down, L0_ffn_se_gate_w):
    import concourse.bacc as bacc
    from concourse.bass_utils import run_bass_kernel_spmd

    def rows(a):
        return np.asarray(a, dtype=np.float32)

    ctxT = rows(ctx_1024).reshape(B * L, D).T
    proj = np.concatenate([rows(L0_xattn_bq)[:, None], rows(L0_xattn_bk)[:, None], rows(L0_xattn_Wq).T,
                           rows(L0_xattn_Wk).T, ctxT], axis=1)
    router = np.concatenate([rows(L0_ffn_gate_w), rows(L0_ffn_se_gate_w), np.zeros((1, L), np.float32)], axis=0)
    router = router.T.reshape(KT, P, R).transpose(1, 0, 2)

    def hidden_blocks(experts, shared):
        w = np.concatenate([rows(experts), rows(shared).reshape(2, P, L)], axis=0)
        return w.reshape(UNITS, P, KT, P).transpose(0, 3, 2, 1).reshape(UNITS, P, KT * P)

    down = np.concatenate([rows(L0_ffn_w_down), rows(L0_ffn_sh_down).reshape(L, 2, P).transpose(1, 0, 2)], axis=0)
    ffn = np.concatenate([hidden_blocks(L0_ffn_w_gate, L0_ffn_sh_gate), hidden_blocks(L0_ffn_w_up, L0_ffn_sh_up),
                          down.transpose(0, 2, 1)], axis=2)

    nc = bacc.Bacc("TRN2", target_bir_lowering=False, num_devices=1)
    arrays = {"proj": proj, "x": rows(x).reshape(B * LT, P, L), "router": router, "ffn": ffn}
    arrays = {name: np.ascontiguousarray(a) for name, a in arrays.items()}
    args = [nc.dram_tensor(name, a.shape, F32, kind="ExternalInput").ap() for name, a in arrays.items()]
    out = nc.dram_tensor("out", (KT, P, B * L), F32, kind="ExternalOutput").ap()
    xattn_moe_kernel(nc, *args, out)
    result = run_bass_kernel_spmd(nc, [arrays], core_ids=[0]).results[0]["out"]
    return np.ascontiguousarray(result.reshape(L, B, L).transpose(1, 2, 0))
```

```python
from contextlib import ExitStack

import numpy as np
import concourse.bass as bass
from concourse import mybir

P = 128
B = 4
L = 256
D = 128
E = 8
LT = L // P
KT = L // P
HB = 2
HT = HB * LT
N = HB * L
UNITS = E + 2
R = E + 2
WU = 3 * KT * P
EPS = 1e-5
RSQRT_SEED = float(0x5F1FFFF9)
RSQRT_A, RSQRT_B = 0.703952253, 2.38924456

F32 = mybir.dt.float32
F32R = mybir.dt.float32r
I32 = mybir.dt.int32
U32 = mybir.dt.uint32
ALU = mybir.AluOpType
ACT = mybir.ActivationFunctionType
AX = mybir.AxisListType


def xattn_moe_kernel(nc, proj, x, router, ffn, out):
    with ExitStack() as ctx:
        def sb(name, shape, dt=F32):
            return ctx.enter_context(nc.sbuf_tensor(name, shape, dt))

        def sem(name):
            return ctx.enter_context(nc.semaphore(name))

        bank = [ctx.enter_context(nc.psum_tensor(f"bank{i}", [P, 512], F32)) for i in range(8)]
        gate_ps, up_ps, comb_ps = bank[0], bank[1], bank[2]
        acc_ps = bank[3:5]

        proj_sb = sb("proj_sb", [P, 2 + 2 * D + B * L])
        x_sb = sb("x_sb", [P, B * LT, L])
        router_sb = sb("router_sb", [P, KT, R])
        router_parts = sb("router_parts", [P, KT, 2, R], F32R)
        ffn_sb = sb("ffn_sb", [P, UNITS, WU])
        ffn_hi = sb("ffn_hi", [P, UNITS, WU], F32R)
        ffn_lo = sb("ffn_lo", [P, UNITS, WU], F32R)
        ident = sb("ident", [P, P])
        zeros = sb("zeros", [P, P])
        iota8 = sb("iota8", [P, HT, E])
        select = sb("select", [P, E + 1, P], F32R)
        qT = sb("qT", [P, B * L])
        kT = sb("kT", [P, B * L])
        stats = sb("stats", [P, B * LT, 6])
        mv = sb("mv", [P, B * LT, 2])
        veps = sb("veps", [P, B * LT])
        seed = sb("seed", [P, B * LT], I32)
        yy = sb("yy", [P, B * LT])
        rstd = sb("rstd", [P, B * LT])
        xln = sb("xln", [P, B * LT, L])
        xlnT = sb("xlnT", [P, B, KT, L])
        nmax = sb("nmax", [P, B * LT])
        psums = sb("psums", [P, B * LT])
        rsum = sb("rsum", [P, B * LT])
        pexp = sb("pexp", [P, B, LT, L])
        probT = sb("probT", [P, B, KT, L])
        x1 = sb("x1", [P, B * LT, L])
        stats2 = sb("stats2", [P, B * LT, 6])
        mv2 = sb("mv2", [P, B * LT, 2])
        rstd2 = sb("rstd2", [P, B * LT])
        xn = xln
        x1T = sb("x1T", [P, KT, B * L])
        xnT_hi = sb("xnT_hi", [P, KT, B * L], F32R)
        xnT_lo = sb("xnT_lo", [P, KT, B * L], F32R)
        score = sb("score", [P, HT, R])
        top = sb("top", [P, HT, 8])
        topi = sb("topi", [P, HT, 8], U32)
        margin = sb("margin", [P, HT, 2])
        tanh_sb = sb("tanh_sb", [P, HT, 2])
        share = sb("share", [P, HT, 3])
        pick0 = sb("pick0", [P, HT, E])
        pick1 = sb("pick1", [P, HT, E])
        comb = sb("comb", [P, HT, E + 1])
        comb_parts = sb("comb_parts", [P, HT, P], F32R)
        combT = sb("combT", [P, 2, N], F32R)
        silu_sb = sb("silu_sb", [P, N])
        weighted = sb("weighted", [P, N])
        act_sb = sb("act_sb", [P, N])
        act_hi = sb("act_hi", [P, 2, N], F32R)
        act_lo = sb("act_lo", [P, 2, N], F32R)

        proj_in = [sem("proj_in0"), sem("proj_in1")]
        x_in = [sem("x_in0"), sem("x_in1")]
        router_in = sem("router_in")
        ffn_in = [sem(f"ffn_in{u}") for u in range(UNITS)]
        const_ready = sem("const_ready")
        pool_step = sem("pool_step")
        router_split = sem("router_split")
        ffn_split = sem("ffn_split")
        qk_ready, qk_stored = sem("qk_ready"), sem("qk_stored")
        xln_ready, xlnT_ready, xlnT_stored = sem("xln_ready"), sem("xlnT_ready"), sem("xlnT_stored")
        energy_ready, nmax_ready, exp_ready = sem("energy_ready"), sem("nmax_ready"), sem("exp_ready")
        prob_ready, probT_ready, probT_stored = sem("prob_ready"), sem("probT_ready"), sem("probT_stored")
        xm_ready, x1_ready, xn_ready = sem("xm_ready"), sem("x1_ready"), sem("xn_ready")
        xnT_ready, xnT_hi_ready, xnT_lo_ready = sem("xnT_ready"), sem("xnT_hi_ready"), sem("xnT_lo_ready")
        x1T_ready, x1T_stored = sem("x1T_ready"), sem("x1T_stored")
        score_ready, margin_ready, tanh_ready = sem("score_ready"), sem("margin_ready"), sem("tanh_ready")
        comb_ready, combT_ready, combT_stored = sem("comb_ready"), sem("combT_ready"), sem("combT_stored")
        cb_ready, gate_ready, up_ready, down_ready = (sem("cb_ready"), sem("gate_ready"), sem("up_ready"),
                                                      sem("down_ready"))
        silu_ready, weighted_ready, act_ready = sem("silu_ready"), sem("weighted_ready"), sem("act_ready")
        act_hi_ready, act_lo_ready = sem("act_hi_ready"), sem("act_lo_ready")
        out_ready, out_stored = sem("out_ready"), sem("out_stored")
        dve_step = sem("dve_step")

        bq, bk = proj_sb[:, 0:1], proj_sb[:, 1:2]
        wqT, wkT = proj_sb[:, 2:2 + D], proj_sb[:, 2 + D:2 + 2 * D]
        C0 = 2 + 2 * D
        ctxT = proj_sb[:, C0:C0 + B * L]

        E_BANK = [bank[6], bank[1], bank[3], bank[4]]
        XLNT_BANK = [bank[5], bank[0], bank[6], bank[7]]
        PT_BANK = [bank[7], bank[2], bank[7], bank[5]]
        XM_BANK = [bank[5], bank[0], bank[5], bank[6]]
        XNT_BANK = [bank[6], bank[1], bank[7], bank[5]]
        X1T_BANK = [bank[7], bank[2], bank[6], bank[7]]
        SCORE_BANK = [bank[5], bank[5]]
        COMBT_BANK = [bank[6], bank[6]]

        def tiles(ps):
            return ps[:, :].rearrange("p (t n) -> p t n", t=2)

        def scores_of(h):
            return SCORE_BANK[h][:, 0:HT * 2 * R].rearrange("p (t r) -> p t r", t=HT)

        def w_of(w, g, kind, k):
            c = (kind * KT + k) * P
            return w[:, g % UNITS, c:c + P]

        block = ctx.enter_context(nc.Block())

        @block.sync
        def _(sp):
            sp.dma_start(proj_sb[:, 0:C0 + N], proj[:, 0:C0 + N]).then_inc(proj_in[0], 16)
            sp.dma_start(proj_sb[:, C0 + N:], proj[:, C0 + N:]).then_inc(proj_in[1], 16)
            sp.dma_start(router_sb[:], router).then_inc(router_in, 16)
            for u in range(UNITS):
                sp.dma_start(ffn_sb[:, u, :], ffn[u]).then_inc(ffn_in[u], 16)
            for h in range(2):
                for k in range(KT):
                    sp.wait_ge(out_ready, h * KT + k + 1)
                    sp.dma_start(out[k, :, h * N:(h + 1) * N], x1T[:, k, h * N:(h + 1) * N]).then_inc(out_stored, 16)
            sp.wait_ge(out_stored, 16 * 2 * KT)

        @block.gpsimd
        def _(pool):
            pool.memset(zeros[:], 0.0).then_inc(pool_step, 1)
            pool.wait_ge(pool_step, 1)
            pool.affine_select(out=ident[:], in_=zeros[:], compare_op=ALU.not_equal, fill=1.0, base=0,
                               pattern=[[-1, P]], channel_multiplier=1)
            pool.iota(iota8[:], pattern=[[0, HT], [1, E]], base=0, channel_multiplier=0,
                      allow_small_or_imprecise_dtypes=True).then_inc(const_ready, 1)
            pool.memset(select[:].bitcast(F32), 0.0)
            pool.memset(comb_parts[:].bitcast(F32), 0.0).then_inc(pool_step, 1)
            pool.wait_ge(pool_step, 2)
            for base in (0, -(E + 1)):
                pool.affine_select(out=select[:], in_=select[:], compare_op=ALU.not_equal, fill=1.0, base=base,
                                   pattern=[[-1, E + 1], [0, P]], channel_multiplier=1).then_inc(pool_step, 1)
                pool.wait_ge(pool_step, 3 if base == 0 else 4)
            pool.wait_ge(router_in, 16)
            pool.tensor_copy(router_parts[:, :, 0], router_sb[:]).then_inc(pool_step, 1)
            pool.wait_ge(pool_step, 5)
            pool.tensor_tensor(router_parts[:, :, 1], router_sb[:], router_parts[:, :, 0].bitcast(F32),
                               ALU.subtract).then_inc(router_split, 1)
            for u in range(UNITS):
                pool.wait_ge(ffn_in[u], 16)
                pool.tensor_copy(ffn_hi[:, u, :], ffn_sb[:, u, :]).then_inc(pool_step, 1)
                pool.wait_ge(pool_step, u + 6)
                pool.tensor_tensor(ffn_lo[:, u, :], ffn_sb[:, u, :], ffn_hi[:, u, :].bitcast(F32),
                                   ALU.subtract).then_inc(ffn_split, 1)

        @block.scalar
        def _(act):
            for h in range(2):
                act.dma_start(x_sb[:, h * HT:(h + 1) * HT, :],
                              x[h * HT:(h + 1) * HT].rearrange("t p n -> p t n")).then_inc(x_in[h], 16)

            def store_qk(h):
                for i, (dst, bias) in enumerate(((qT, bq), (kT, bk))):
                    act.wait_ge(qk_ready, 2 * h + i + 1)
                    act.activation(dst[:, h * N:(h + 1) * N], acc_ps[i][:, :], ACT.Identity,
                                   bias=bias).then_inc(qk_stored, 1)

            def store_xlnT(b):
                act.wait_ge(xlnT_ready, b + 1)
                act.copy(xlnT[:, b], tiles(XLNT_BANK[b])).then_inc(xlnT_stored, 1)

            def exps(b):
                act.wait_ge(nmax_ready, b + 1)
                for t in range(LT):
                    i = b * LT + t
                    last = act.activation(pexp[:, b, t, :], tiles(E_BANK[b])[:, t, :], ACT.Exp,
                                          bias=nmax[:, i:i + 1], accum_out=psums[:, i:i + 1])
                last.then_inc(exp_ready, 1)

            def store_probT(b):
                act.wait_ge(probT_ready, b + 1)
                act.copy(probT[:, b], tiles(PT_BANK[b])).then_inc(probT_stored, 1)

            def store_xnT_hi(b):
                act.wait_ge(xnT_ready, b + 1)
                act.copy(xnT_hi[:, :, b * L:(b + 1) * L], tiles(XNT_BANK[b])).then_inc(xnT_hi_ready, 1)

            def store_x1T(b):
                act.wait_ge(x1T_ready, b + 1)
                act.copy(x1T[:, :, b * L:(b + 1) * L], tiles(X1T_BANK[b])).then_inc(x1T_stored, 1)

            def routing_tanh(h):
                act.wait_ge(margin_ready, h + 1)
                act.activation(tanh_sb[:], margin[:], ACT.Tanh, scale=0.5).then_inc(tanh_ready, 1)

            def store_combT(h):
                act.wait_ge(combT_ready, h + 1)
                act.copy(combT[:, h], COMBT_BANK[h][:, :]).then_inc(combT_stored, 1)

            store_qk(0)
            for b in range(HB):
                exps(b)
                store_xlnT(b)
            store_qk(1)
            for b in range(HB):
                store_probT(b)
            for b in range(HB):
                store_xnT_hi(b)
            for b in range(HB, B):
                exps(b)
            for b in range(HB):
                store_x1T(b)
            between = {0: [(routing_tanh, 0), (store_combT, 0)],
                       1: [(store_probT, 2), (store_probT, 3)], 2: [(store_xlnT, 2), (store_xlnT, 3)],
                       7: [(store_xnT_hi, 2), (store_xnT_hi, 3), (store_x1T, 2)],
                       8: [(store_x1T, 3), (routing_tanh, 1)], 9: [(store_combT, 1)]}
            for g in range(2 * UNITS):
                act.wait_ge(gate_ready, g + 1)
                if g >= 1:
                    act.wait_ge(weighted_ready, g)
                act.activation(silu_sb[:], gate_ps[:, :], ACT.Silu).then_inc(silu_ready, 1)
                if g == 0:
                    for step, i in between[0]:
                        step(i)
                act.wait_ge(act_ready, g + 1)
                if g >= 2:
                    act.wait_ge(down_ready, g - 1)
                act.copy(act_hi[:, g % 2, :], act_sb[:]).then_inc(act_hi_ready, 1)
                if g:
                    for step, i in between.get(g, []):
                        step(i)

        @block.vector
        def _(dve):
            count = [0]

            def then(ins):
                count[0] += 1
                ins.then_inc(dve_step, 1)
                dve.wait_ge(dve_step, count[0])

            def rsqrt(y, var, n0, n1):
                v, s, t = veps[:, n0:n1], seed[:, n0:n1], yy[:, n0:n1]
                then(dve.tensor_scalar(v, var, EPS, None, ALU.add))
                then(dve.tensor_scalar(s, v.bitcast(I32), 1, None, ALU.logical_shift_right))
                then(dve.tensor_scalar(y.bitcast(I32), s, -1.0, RSQRT_SEED, ALU.mult, ALU.add))
                for a, c in ((-RSQRT_A, RSQRT_A * RSQRT_B), (-0.5, 1.5)):
                    then(dve.scalar_tensor_tensor(t, y, a, y, ALU.mult, ALU.mult))
                    then(dve.tensor_tensor(t, t, v, ALU.mult))
                    then(dve.scalar_tensor_tensor(y, t, c, y, ALU.add, ALU.mult))

            def moments(src, st, m, i):
                dve.bn_stats(st[:, i, :], src[:, i, :])

            def norm1_stats(h):
                dve.wait_ge(x_in[h], 16)
                for i in range(h * HT, (h + 1) * HT):
                    last = dve.bn_stats(stats[:, i, :], x_sb[:, i, :])
                then(last)
                for i in range(h * HT, (h + 1) * HT):
                    last = dve.bn_aggr(mv[:, i, :], stats[:, i, :])
                then(last)
                rsqrt(rstd[:, h * HT:(h + 1) * HT], mv[:, h * HT:(h + 1) * HT, 1], h * HT, (h + 1) * HT)

            def norm1(b):
                for i in range(b * LT, (b + 1) * LT):
                    last = dve.tensor_scalar(xln[:, i, :], x_sb[:, i, :], mv[:, i, 0:1], rstd[:, i:i + 1],
                                             ALU.subtract, ALU.mult)
                last.then_inc(xln_ready, 1)

            def row_max(b):
                dve.wait_ge(energy_ready, b + 1)
                dve.reduce_max(nmax[:, b * LT:(b + 1) * LT], tiles(E_BANK[b]), AX.X,
                               negate=True).then_inc(nmax_ready, 1)

            def normalise(b):
                dve.wait_ge(exp_ready, b + 1)
                then(dve.reciprocal(rsum[:, b * LT:(b + 1) * LT], psums[:, b * LT:(b + 1) * LT]))
                for t in range(LT):
                    i = b * LT + t
                    last = dve.tensor_scalar(pexp[:, b, t, :], pexp[:, b, t, :], rsum[:, i:i + 1], None, ALU.mult)
                last.then_inc(prob_ready, 1)

            def add_attention(b):
                dve.wait_ge(xm_ready, b + 1)
                dve.tensor_tensor(x1[:, b * LT:(b + 1) * LT, :], tiles(XM_BANK[b]),
                                  x_sb[:, b * LT:(b + 1) * LT, :], ALU.add).then_inc(x1_ready, 1)

            def norm2_stats(b):
                dve.wait_ge(x1_ready, b + 1)
                for i in range(b * LT, (b + 1) * LT):
                    last = dve.bn_stats(stats2[:, i, :], x1[:, i, :])
                then(last)
                for i in range(b * LT, (b + 1) * LT):
                    last = dve.bn_aggr(mv2[:, i, :], stats2[:, i, :])
                then(last)

            def norm2(h):
                n0, n1 = h * HT, (h + 1) * HT
                rsqrt(rstd2[:, n0:n1], mv2[:, n0:n1, 1], n0, n1)
                for i in range(n0, n1):
                    last = dve.tensor_scalar(xn[:, i, :], x1[:, i, :], mv2[:, i, 0:1], rstd2[:, i:i + 1],
                                             ALU.subtract, ALU.mult)
                    if i % LT == LT - 1:
                        last.then_inc(xn_ready, 1)

            def store_xnT_lo(b):
                dve.wait_ge(xnT_hi_ready, b + 1)
                cols = slice(b * L, (b + 1) * L)
                dve.tensor_tensor(xnT_lo[:, :, cols], tiles(XNT_BANK[b]), xnT_hi[:, :, cols].bitcast(F32),
                                  ALU.subtract).then_inc(xnT_lo_ready, 1)

            def top_two(h):
                dve.wait_ge(score_ready, h + 1)
                then(dve.tensor_reduce(score[:], scores_of(h).rearrange("p t (i r) -> p t r i", i=2), AX.X, ALU.add))
                for t in range(HT):
                    dve.max(top[:, t, :], score[:, t, 0:E])
                then(dve.tensor_copy(margin[:, :, 1], score[:, :, E]))
                dve.tensor_tensor(margin[:, :, 0], top[:, :, 0], top[:, :, 1],
                                  ALU.subtract).then_inc(margin_ready, 1)
                for t in range(HT):
                    last = dve.max_index(topi[:, t, :], top[:, t, :], score[:, t, 0:E])
                then(last)

            def combine(h):
                for i, pick in enumerate((pick0, pick1)):
                    dve.tensor_tensor(pick[:], iota8[:], topi[:, :, i:i + 1].broadcast_to([P, HT, E]), ALU.is_equal)
                dve.wait_ge(tanh_ready, h + 1)
                dve.tensor_scalar(share[:, :, 0:2], tanh_sb[:], 0.5, 0.5, ALU.mult, ALU.add)
                then(dve.tensor_scalar(share[:, :, 2], tanh_sb[:, :, 0], -0.5, 0.5, ALU.mult, ALU.add))
                for i, pick in ((0, pick0), (2, pick1)):
                    last = dve.tensor_tensor(pick[:], pick[:], share[:, :, i:i + 1].broadcast_to([P, HT, E]), ALU.mult)
                then(last)
                dve.tensor_copy(comb[:, :, E], share[:, :, 1])
                then(dve.tensor_tensor(comb[:, :, 0:E], pick0[:], pick1[:], ALU.add))
                then(dve.tensor_copy(comb_parts[:, :, 0:E + 1], comb[:]))
                dve.tensor_tensor(comb_parts[:, :, E + 1:2 * (E + 1)], comb[:],
                                  comb_parts[:, :, 0:E + 1].bitcast(F32), ALU.subtract).then_inc(comb_ready, 1)

            def finish(h):
                dve.wait_ge(down_ready, (h + 1) * UNITS)
                dve.wait_ge(x1T_stored, (h + 1) * HB)
                for k in range(KT):
                    rows = x1T[:, k, h * N:(h + 1) * N]
                    dve.tensor_tensor(rows, acc_ps[k][:, :], rows, ALU.add).then_inc(out_ready, 1)

            dve.wait_ge(const_ready, 1)
            norm1_stats(0)
            row_max(0)
            row_max(1)
            norm1(0)
            norm1(1)
            normalise(0)
            normalise(1)
            for b in range(HB):
                add_attention(b)
                norm2_stats(b)
            norm2(0)
            for b in range(HB, B):
                row_max(b)
            for b in range(HB):
                store_xnT_lo(b)
            top_two(0)
            combine(0)
            for b in range(HB, B):
                normalise(b)
            between = {0: [(norm1_stats, 1)], 1: [(norm1, 2), (norm1, 3)],
                       3: [(add_attention, 2), (add_attention, 3)], 4: [(norm2_stats, 2), (norm2_stats, 3)],
                       5: [(norm2, 1)], 7: [(store_xnT_lo, 2), (store_xnT_lo, 3)],
                       8: [(top_two, 1), (combine, 1)], UNITS: [(finish, 0)]}
            for g in range(2 * UNITS):
                dve.wait_ge(silu_ready, g + 1)
                dve.wait_ge(cb_ready, g + 1)
                dve.tensor_tensor(weighted[:], comb_ps[:, :], silu_sb[:], ALU.mult).then_inc(weighted_ready, 1)
                dve.wait_ge(weighted_ready, g + 1)
                dve.wait_ge(up_ready, g + 1)
                dve.tensor_tensor(act_sb[:], up_ps[:, :], weighted[:], ALU.mult).then_inc(act_ready, 1)
                dve.wait_ge(act_hi_ready, g + 1)
                dve.tensor_tensor(act_lo[:, g % 2, :], act_sb[:], act_hi[:, g % 2, :].bitcast(F32),
                                  ALU.subtract).then_inc(act_lo_ready, 1)
                for step, i in between.get(g, []):
                    step(i)
            finish(1)

        @block.tensor
        def _(pe):
            def project(h):
                for i, w in enumerate((wqT, wkT)):
                    if h:
                        pe.wait_ge(qk_stored, i + 1)
                    pe.matmul(acc_ps[i][:, :], w, ctxT[:, h * N:(h + 1) * N], start=True,
                              stop=True).then_inc(qk_ready, 1)

            def transpose4(dst, src):
                for k in range(KT):
                    for t in range(LT):
                        last = pe.transpose(dst[:, k, t * P:(t + 1) * P], src[:, t, k * P:(k + 1) * P], ident[:])
                return last

            def energy(b):
                pe.wait_ge(qk_stored, 2 * (b // HB) + 2)
                for t in range(LT):
                    n = b * L + t * P
                    last = pe.matmul(tiles(E_BANK[b])[:, t, :], qT[:, n:n + P], kT[:, b * L:(b + 1) * L],
                                     start=True, stop=True)
                last.then_inc(energy_ready, 1)

            def transpose_xln(b):
                pe.wait_ge(xln_ready, b + 1)
                transpose4(tiles(XLNT_BANK[b]), xln[:, b * LT:(b + 1) * LT, :]).then_inc(xlnT_ready, 1)

            def transpose_prob(b):
                pe.wait_ge(prob_ready, b + 1)
                transpose4(tiles(PT_BANK[b]), pexp[:, b]).then_inc(probT_ready, 1)

            def attend(b):
                pe.wait_ge(xlnT_stored, b + 1)
                pe.wait_ge(probT_stored, b + 1)
                for t in range(LT):
                    for k in range(KT):
                        last = pe.matmul(tiles(XM_BANK[b])[:, t, :], xlnT[:, b, k, t * P:(t + 1) * P],
                                         probT[:, b, k, :], start=(k == 0), stop=(k == KT - 1))
                last.then_inc(xm_ready, 1)

            def transpose_xn(b):
                pe.wait_ge(xn_ready, b + 1)
                transpose4(tiles(XNT_BANK[b]), xn[:, b * LT:(b + 1) * LT, :]).then_inc(xnT_ready, 1)

            def transpose_x1(b):
                transpose4(tiles(X1T_BANK[b]), x1[:, b * LT:(b + 1) * LT, :]).then_inc(x1T_ready, 1)

            def route(h):
                pe.wait_ge(router_split, 1)
                pe.wait_ge(xnT_lo_ready, (h + 1) * HB)
                for t in range(HT):
                    cols = slice(h * N + t * P, h * N + (t + 1) * P)
                    parts = [(a, k) for k in range(KT) for a in (xnT_lo, xnT_hi)]
                    for i, (a, k) in enumerate(parts):
                        last = pe.matmul(scores_of(h)[:, t, :], a[:, k, cols],
                                         router_parts[:, k].rearrange("p i r -> p (i r)"),
                                         start=(i == 0), stop=(i == len(parts) - 1))
                last.then_inc(score_ready, 1)

            def transpose_comb(h):
                pe.wait_ge(comb_ready, h + 1)
                for t in range(HT):
                    last = pe.transpose(COMBT_BANK[h][:, t * P:(t + 1) * P], comb_parts[:, t, :].bitcast(F32),
                                        ident[:])
                last.then_inc(combT_ready, 1)

            def weights_of_tokens(g):
                pe.wait_ge(combT_stored, g // UNITS + 1)
                if g >= 1:
                    pe.wait_ge(weighted_ready, g)
                pe.matmul(comb_ps[:, :], select[:, min(g % UNITS, E), :], combT[:, g // UNITS], start=True,
                          stop=True).then_inc(cb_ready, 1)

            def hidden(g, kind, ps):
                cols = slice(g // UNITS * N, (g // UNITS + 1) * N)
                parts = [(w, a, k) for k in range(KT) for w, a in
                         ((ffn_hi, xnT_hi), (ffn_hi, xnT_lo), (ffn_lo, xnT_hi))]
                for i, (w, a, k) in enumerate(parts):
                    last = pe.matmul(ps[:, :], w_of(w, g, kind, k), a[:, k, cols],
                                     start=(i == 0), stop=(i == len(parts) - 1))
                return last

            def down(g):
                if g == 0:
                    pe.wait_ge(exp_ready, B)
                if g == UNITS:
                    pe.wait_ge(out_ready, KT)
                for parts, ready in ((((ffn_hi, act_hi), (ffn_lo, act_hi)), act_hi_ready),
                                     (((ffn_hi, act_lo),), act_lo_ready)):
                    pe.wait_ge(ready, g + 1)
                    for k in range(KT):
                        for w, a in parts:
                            last = pe.matmul(acc_ps[k][:, :], w_of(w, g, 2, k), a[:, g % 2, :],
                                             start=(g % UNITS == 0 and w is ffn_hi and a is act_hi),
                                             stop=(g % UNITS == UNITS - 1 and a is act_lo))
                last.then_inc(down_ready, 1)

            pe.wait_ge(proj_in[0], 16)
            project(0)
            for b in range(HB):
                energy(b)
            pe.wait_ge(const_ready, 1)
            for b in range(HB):
                transpose_xln(b)
            pe.wait_ge(proj_in[1], 16)
            project(1)
            for b in range(HB):
                transpose_prob(b)
            for b in range(HB):
                attend(b)
            pe.wait_ge(qk_stored, 4)
            for b in range(HB, B):
                energy(b)
            for b in range(HB):
                transpose_xn(b)
            for b in range(HB):
                transpose_x1(b)
            route(0)

            def before_second(step, b):
                if (step, b) == (transpose_prob, 2):
                    pe.wait_ge(x1T_stored, 1)
                elif (step, b) == (transpose_prob, 3):
                    pe.wait_ge(margin_ready, 1)
                elif (step, b) == (transpose_xln, 2):
                    pe.wait_ge(combT_stored, 1)
                elif (step, b) == (transpose_xln, 3):
                    pe.wait_ge(probT_stored, 3)
                elif (step, b) == (attend, 2):
                    pe.wait_ge(probT_stored, 4)
                elif (step, b) == (attend, 3):
                    pe.wait_ge(xlnT_stored, 3)
                elif (step, b) == (transpose_xn, 2):
                    pe.wait_ge(xlnT_stored, 4)
                elif (step, b) == (transpose_xn, 3):
                    pe.wait_ge(x1_ready, 3)
                elif (step, b) == (transpose_x1, 2):
                    pe.wait_ge(x1_ready, 4)
                elif (step, b) == (transpose_x1, 3):
                    pe.wait_ge(xnT_lo_ready, 3)
                elif (step, b) == (transpose_comb, 1):
                    pe.wait_ge(x1T_stored, 3)

            between = {1: [(transpose_prob, 2), (transpose_prob, 3)],
                       2: [(transpose_xln, 2), (transpose_xln, 3)], 3: [(attend, 2), (attend, 3)],
                       7: [(transpose_xn, 2), (transpose_xn, 3), (transpose_x1, 2)],
                       8: [(transpose_x1, 3), (route, 1)], 9: [(transpose_comb, 1)]}
            for g in range(2 * UNITS):
                if g < UNITS:
                    pe.wait_ge(ffn_split, g + 1)
                if g >= 1:
                    pe.wait_ge(silu_ready, g)
                hidden(g, 0, gate_ps).then_inc(gate_ready, 1)
                if g >= 1:
                    weights_of_tokens(g)
                    pe.wait_ge(act_ready, g)
                hidden(g, 1, up_ps).then_inc(up_ready, 1)
                if g == 0:
                    transpose_comb(0)
                    weights_of_tokens(0)
                for step, i in between.get(g, []):
                    before_second(step, i)
                    step(i)
                if g >= 1:
                    down(g - 1)
            down(2 * UNITS - 1)


def kernel(x, ctx_1024, L0_xattn_Wq, L0_xattn_bq, L0_xattn_Wk, L0_xattn_bk, L0_ffn_gate_w, L0_ffn_w_gate,
           L0_ffn_w_up, L0_ffn_w_down, L0_ffn_sh_gate, L0_ffn_sh_up, L0_ffn_sh_down, L0_ffn_se_gate_w):
    import concourse.bacc as bacc
    from concourse.bass_utils import run_bass_kernel_spmd

    def rows(a):
        return np.asarray(a, dtype=np.float32)

    ctxT = rows(ctx_1024).reshape(B * L, D).T
    proj = np.concatenate([rows(L0_xattn_bq)[:, None], rows(L0_xattn_bk)[:, None], rows(L0_xattn_Wq).T,
                           rows(L0_xattn_Wk).T, ctxT], axis=1)
    router = np.concatenate([rows(L0_ffn_gate_w), rows(L0_ffn_se_gate_w), np.zeros((1, L), np.float32)], axis=0)
    router = router.T.reshape(KT, P, R).transpose(1, 0, 2)

    def hidden_blocks(experts, shared):
        w = np.concatenate([rows(experts), rows(shared).reshape(2, P, L)], axis=0)
        return w.reshape(UNITS, P, KT, P).transpose(0, 3, 2, 1).reshape(UNITS, P, KT * P)

    down = np.concatenate([rows(L0_ffn_w_down), rows(L0_ffn_sh_down).reshape(L, 2, P).transpose(1, 0, 2)], axis=0)
    ffn = np.concatenate([hidden_blocks(L0_ffn_w_gate, L0_ffn_sh_gate), hidden_blocks(L0_ffn_w_up, L0_ffn_sh_up),
                          down.transpose(0, 2, 1)], axis=2)

    nc = bacc.Bacc("TRN2", target_bir_lowering=False, num_devices=1)
    arrays = {"proj": proj, "x": rows(x).reshape(B * LT, P, L), "router": router, "ffn": ffn}
    arrays = {name: np.ascontiguousarray(a) for name, a in arrays.items()}
    args = [nc.dram_tensor(name, a.shape, F32, kind="ExternalInput").ap() for name, a in arrays.items()]
    out = nc.dram_tensor("out", (KT, P, B * L), F32, kind="ExternalOutput").ap()
    xattn_moe_kernel(nc, *args, out)
    result = run_bass_kernel_spmd(nc, [arrays], core_ids=[0]).results[0]["out"]
    return np.ascontiguousarray(result.reshape(L, B, L).transpose(1, 2, 0))
```

```python
from contextlib import ExitStack

import numpy as np
import concourse.bass as bass
from concourse import mybir

P = 128
B = 4
L = 256
D = 128
E = 8
LT = L // P
KT = L // P
HB = 2
HT = HB * LT
N = HB * L
SH = 2
UNITS = SH + E
R = E + 2
WU = 3 * KT * P
EPS = 1e-5
WARM0, WARM = 7, 6
SPLIT0 = 4
SLOTS = 4
ROWS = 32
RSQRT_SEED = float(0x5F1FFFF9)
RSQRT_STEPS = 9
RSQRT_A, RSQRT_B = 0.703952253, 2.38924456

F32 = mybir.dt.float32
F32R = mybir.dt.float32r
I32 = mybir.dt.int32
U32 = mybir.dt.uint32
ALU = mybir.AluOpType
ACT = mybir.ActivationFunctionType
AX = mybir.AxisListType


def xattn_moe_kernel(nc, proj, x, router, ffn, comb_dram, out):
    with ExitStack() as ctx:
        def sb(name, shape, dt=F32):
            return ctx.enter_context(nc.sbuf_tensor(name, shape, dt))

        def sem(name):
            return ctx.enter_context(nc.semaphore(name))

        bank = [ctx.enter_context(nc.psum_tensor(f"bank{i}", [P, 512], F32)) for i in range(8)]
        gate_ps, comb_ps, warm_ps = bank[0], bank[2], bank[0]
        acc_ps = bank[3:5]

        proj_sb = sb("proj_sb", [P, 2 + 2 * D + B * L])
        x_sb = sb("x_sb", [P, B * LT, L])
        router_sb = sb("router_sb", [P, KT, R])
        router_parts = sb("router_parts", [P, KT, 2, R], F32R)
        ffn_sb = sb("ffn_sb", [P, SLOTS, WU])
        ffn_hi = sb("ffn_hi", [P, UNITS, WU], F32R)
        ffn_lo = sb("ffn_lo", [P, UNITS, WU], F32R)
        ident = sb("ident", [P, P])
        zeros = sb("zeros", [P, P])
        warm = sb("warm", [P, N], mybir.dt.bfloat16)
        iota8 = sb("iota8", [P, HT, E])
        select = sb("select", [P, P], F32R)
        qT = sb("qT", [P, B * L])
        kT = sb("kT", [P, B * L])
        stats = sb("stats", [P, B * LT, 6])
        mv = sb("mv", [P, B * LT, 2])
        veps = sb("veps", [P, B * LT])
        seed = sb("seed", [P, B * LT], I32)
        yy = sb("yy", [P, B * LT])
        rstd = sb("rstd", [P, B * LT])
        xc = sb("xc", [P, B * LT, L])
        nmean = sb("nmean", [P, LT])
        xcT = sb("xcT", [P, HB, KT, L])
        xcT_hi = sb("xcT_hi", [P, HB, KT, L], F32R)
        xcT_lo = sb("xcT_lo", [P, HB, KT, L], F32R)
        nmax = sb("nmax", [P, B * LT])
        psums = sb("psums", [P, B * LT])
        rsum = sb("rsum", [P, B * LT])
        pexp = sb("pexp", [P, B, LT, L])
        probT_hi = sb("probT_hi", [P, HB, KT, L], F32R)
        probT_lo = sb("probT_lo", [P, HB, KT, L], F32R)
        x1 = sb("x1", [P, B * LT, L])
        stats2 = sb("stats2", [P, B * LT, 6])
        mv2 = sb("mv2", [P, B * LT, 2])
        rstd2 = sb("rstd2", [P, B * LT])
        xn = xc
        x1T = sb("x1T", [P, KT, B * L])
        xnT_hi = sb("xnT_hi", [P, KT, B * L], F32R)
        xnT_lo = sb("xnT_lo", [P, KT, B * L], F32R)
        score = sb("score", [P, HT, R])
        top = sb("top", [P, HT, 8])
        topi = sb("topi", [P, HT, 8], U32)
        margin = sb("margin", [P, HT, 2])
        tanh_sb = sb("tanh_sb", [P, HT, 2])
        unread, unread_in = sb("unread", [P, 1]), sb("unread_in", [P, 1])
        share = sb("share", [P, HT])
        pick0 = sb("pick0", [P, HT, E])
        pick1 = sb("pick1", [P, HT, E])
        differ = sb("differ", [P, HT, E])
        comb_parts = sb("comb_parts", [P, HT, P], F32R)
        combT = sb("combT", [P, N], F32R)
        comb_rows = sb("comb_rows", [P, 2, N])
        comb_all = sb("comb_all", [P, E + 1, N])
        silu_sb = sb("silu_sb", [P, 2, N])
        probT = silu_sb[:, 0, :].rearrange("p (k n) -> p k n", k=KT)
        weighted = sb("weighted", [P, N])
        act_sb = sb("act_sb", [P, N])
        act_hi = sb("act_hi", [P, 2, N], F32R)
        act_lo = sb("act_lo", [P, 2, N], F32R)

        proj_in = [sem("proj_in0"), sem("proj_in1"), sem("proj_in23")]
        x_in = [sem(f"x_in{b}") for b in range(B)]
        router_in = sem("router_in")
        ffn_in = [sem(f"ffn_in{u}") for u in range(UNITS)]
        const_ready = sem("const_ready")
        pool_step = sem("pool_step")
        router_split = sem("router_split")
        ffn_hi_ready = sem("ffn_hi_ready")
        ffn_split = sem("ffn_split")
        warm_ready, mean_ready = sem("warm_ready"), sem("mean_ready")
        qk_ready, q_stored, k_stored = sem("qk_ready"), sem("q_stored"), sem("k_stored")
        xc_ready = [sem(f"xc_ready{b}") for b in range(B)]
        xcT_ready, xcT_hi_ready = sem("xcT_ready"), sem("xcT_hi_ready")
        energy_ready, nmax_ready, exp_ready = sem("energy_ready"), sem("nmax_ready"), sem("exp_ready")
        prob_ready, probT_ready, probT_hi_ready = sem("prob_ready"), sem("probT_ready"), sem("probT_hi_ready")
        xcT_stored = {b: sem(f"xcT_stored{b}") for b in (0, 2, 3)}
        xcT_lo_ready = {b: sem(f"xcT_lo_ready{b}") for b in (0, 2, 3)}
        probT_lo_ready, nmean_ready = sem("probT_lo_ready"), sem("nmean_ready")
        xm_ready, x1_ready = sem("xm_ready"), sem("x1_ready")
        mean2_ready, x1c_ready, rsqrt_step = sem("mean2_ready"), sem("x1c_ready"), sem("rsqrt_step")
        xn_ready = [sem("xn_ready0"), sem("xn_ready1")]
        xnT_ready, xnT_hi_ready, xnT_lo_ready = sem("xnT_ready"), sem("xnT_hi_ready"), sem("xnT_lo_ready")
        x1T_ready, x1T_stored = sem("x1T_ready"), sem("x1T_stored")
        score_ready, margin_ready, tanh_ready = sem("score_ready"), sem("margin_ready"), sem("tanh_ready")
        comb_ready, combT_ready, combT_stored = sem("comb_ready"), sem("combT_ready"), sem("combT_stored")
        rows_stored, rows_saved = sem("rows_stored"), sem("rows_saved")
        comb_in = [sem(f"comb_in{e}") for e in range(E + 1)]
        cb_ready, gate_ready, up_ready, down_ready = (sem("cb_ready"), sem("gate_ready"), sem("up_ready"),
                                                      sem("down_ready"))
        sums_ready = sem("sums_ready")
        silu_ready, weighted_ready, act_ready = sem("silu_ready"), sem("weighted_ready"), sem("act_ready")
        act_hi_ready, act_lo_ready = sem("act_hi_ready"), sem("act_lo_ready")
        out_ready, out_stored = sem("out_ready"), sem("out_stored")
        dve_step = sem("dve_step")

        bq, bk = proj_sb[:, 0:1], proj_sb[:, 1:2]
        wqT, wkT = proj_sb[:, 2:2 + D], proj_sb[:, 2 + D:2 + 2 * D]
        C0 = 2 + 2 * D
        ctxT = proj_sb[:, C0:C0 + B * L]

        Q_BANK = [bank[3], bank[0], bank[3]]
        K_BANK = [bank[4], bank[2], bank[4]]
        UP_BANK = [bank[1], bank[7]] + [bank[2 - g % 2] for g in range(2, 2 * UNITS)]
        E_BANK = [bank[6], bank[1], bank[3], bank[4]]
        XCT_BANK = [bank[5], bank[0], bank[7], bank[5]]
        PT_BANK = [bank[7], bank[2], bank[4], bank[5]]
        XM_BANK = [bank[5], bank[0], bank[5], bank[6]]
        XNT_BANK = [bank[6], bank[1], bank[7], bank[5]]
        X1T_BANK = [bank[7], bank[2], bank[6], bank[7]]
        SCORE_BANK, COMBT_BANK = bank[5], bank[6]

        scores_ps = SCORE_BANK[:, 0:HT * 2 * R].rearrange("p (t r) -> p t r", t=HT)
        CTX = [(0, L), (L, N), (N, B * L)]

        def columns(g):
            return [slice(0, N)] if g < 2 * UNITS - 1 else [slice(0, L), slice(L, N)]

        def turn(b):
            return b + 1 - 2 * (b % HB)

        def rsqrt_steps(norm, h, n):
            return (2 * h + norm - 1) * RSQRT_STEPS + n

        def tiles(ps):
            return ps[:, :].rearrange("p (t n) -> p t n", t=2)

        def w_of(w, g, kind, k):
            c = (kind * KT + k) * P
            return w[:, g % UNITS, c:c + P]

        def store_out(engine, h, k):
            cols = slice(h * N, (h + 1) * N)
            engine.wait_ge(out_ready, h * KT + k + 1)
            engine.dma_start(out[k, :, cols], x1T[:, k, cols]).then_inc(out_stored, 16)

        block = ctx.enter_context(nc.Block())

        @block.sync
        def _(sp):
            def save_rows(h):
                sp.wait_ge(rows_stored, h + 1)
                sp.dma_start(comb_dram[h], comb_rows[ROWS:ROWS + E + 1, h, :]).then_inc(rows_saved, 16)

            def spread_row(h, e):
                sp.wait_ge(rows_saved, 16 * (h + 1))
                sp.dma_start(comb_all[:, e, :], comb_dram[h, e:e + 1, :].broadcast_to([P, N])).then_inc(comb_in[e], 16)

            for i, (c0, c1) in enumerate(((0, C0 + L), (C0 + L, C0 + N), (C0 + N, C0 + B * L))):
                if i == 2:
                    sp.dma_start(router_sb[:], router).then_inc(router_in, 16)
                sp.dma_start(proj_sb[:, c0:c1], proj[:, c0:c1]).then_inc(proj_in[i], 16)
            for u in range(UNITS):
                if u >= SLOTS:
                    sp.wait_ge(ffn_split, u - SLOTS + 1)
                sp.dma_start(ffn_sb[:, u % SLOTS, :], ffn[u]).then_inc(ffn_in[u], 16)
                if u == SLOTS + 1:
                    save_rows(0)
                elif u == SLOTS + 2:
                    for e in range(E):
                        spread_row(0, e)
            save_rows(1)
            spread_row(1, E)
            for e in range(E):
                sp.wait_ge(weighted_ready, SH + e + 1)
                spread_row(1, e)
            store_out(sp, 0, 0)
            store_out(sp, 0, 1)
            store_out(sp, 1, 0)
            sp.wait_ge(out_stored, 16 * 2 * KT)

        @block.gpsimd
        def _(pool):
            def center(b):
                pool.wait_ge(mean_ready, b + 1)
                for i in range(b * LT, (b + 1) * LT):
                    last = pool.tensor_scalar(xc[:, i, :], x_sb[:, i, :], mv[:, i, 0:1], None, ALU.subtract)
                last.then_inc(xc_ready[b], 1)

            def store_xcT_lo(b):
                pool.wait_ge(xcT_stored[b], 1)
                pool.tensor_tensor(xcT_lo[:, b % HB], xcT[:, b % HB], xcT_hi[:, b % HB].bitcast(F32),
                                   ALU.subtract).then_inc(xcT_lo_ready[b], 1)

            def demean(b):
                pool.wait_ge(mean2_ready, b + 1)
                for i in range(b * LT, (b + 1) * LT):
                    last = pool.tensor_scalar(xn[:, i, :], x1[:, i, :], mv2[:, i, 0:1], None, ALU.subtract)
                last.then_inc(x1c_ready, 1)

            pool.memset(zeros[:], 0.0).then_inc(pool_step, 1)
            pool.wait_ge(pool_step, 1)
            pool.affine_select(out=ident[:], in_=zeros[:], compare_op=ALU.not_equal, fill=1.0, base=0,
                               pattern=[[-1, P]], channel_multiplier=1)
            pool.iota(iota8[:], pattern=[[0, HT], [1, E]], base=0, channel_multiplier=0,
                      allow_small_or_imprecise_dtypes=True).then_inc(const_ready, 1)
            pool.memset(select[:].bitcast(F32), 0.0)
            pool.memset(comb_parts[:].bitcast(F32), 0.0).then_inc(pool_step, 1)
            pool.wait_ge(pool_step, 2)
            for base in (-E, -(2 * E + 1)):
                pool.affine_select(out=select[:], in_=select[:], compare_op=ALU.not_equal, fill=1.0, base=base,
                                   pattern=[[0, P]], channel_multiplier=1).then_inc(pool_step, 1)
                pool.wait_ge(pool_step, 3 if base == -E else 4)
            center(0)
            center(1)
            pool.wait_ge(router_in, 16)
            pool.tensor_copy(router_parts[:, :, 0], router_sb[:]).then_inc(pool_step, 1)
            pool.wait_ge(pool_step, 5)
            pool.tensor_tensor(router_parts[:, :, 1], router_sb[:], router_parts[:, :, 0].bitcast(F32),
                               ALU.subtract).then_inc(router_split, 1)
            store_xcT_lo(0)
            center(2)
            demean(0)
            for u in range(UNITS):
                pool.wait_ge(ffn_hi_ready, u + 1)
                pool.tensor_tensor(ffn_lo[:, u, :], ffn_sb[:, u % SLOTS, :], ffn_hi[:, u, :].bitcast(F32),
                                   ALU.subtract).then_inc(ffn_split, 1)
                if u == 0:
                    store_xcT_lo(2)
                    store_xcT_lo(3)
                elif u == 6:
                    demean(2)

        @block.scalar
        def _(act):
            for b in range(B):
                tiles_b = slice(b * LT, (b + 1) * LT)
                act.dma_start(x_sb[:, tiles_b, :], x[tiles_b].rearrange("t p n -> p t n")).then_inc(x_in[b], 16)

            def store(dst, bias, i, ps, stored, which):
                cols = slice(*CTX[i])
                act.wait_ge(qk_ready, 2 * i + which + 1)
                act.activation(dst[:, cols], ps[:, 0:CTX[i][1] - CTX[i][0]], ACT.Identity,
                               bias=bias).then_inc(stored, 1)

            def store_q(i):
                store(qT, bq, i, Q_BANK[i], q_stored, 0)

            def store_k(i):
                store(kT, bk, i, K_BANK[i], k_stored, 1)

            def split_hi(u):
                act.wait_ge(ffn_in[u], 16)
                act.copy(ffn_hi[:, u, :], ffn_sb[:, u % SLOTS, :]).then_inc(ffn_hi_ready, 1)

            def store_xcT(b):
                act.wait_ge(xcT_ready, b + 1)
                if b >= HB:
                    act.wait_ge(xm_ready, b - HB + 1)
                part = xcT[:, 1] if b == 1 else xcT_hi[:, b % HB]
                act.copy(part, tiles(XCT_BANK[b])).then_inc(xcT_hi_ready, 1)

            def store_plain_xcT(b):
                act.wait_ge(xcT_ready, b + 1)
                if b == 2:
                    act.wait_ge(xcT_lo_ready[0], 1)
                elif b == 3:
                    act.wait_ge(xm_ready, 2)
                act.copy(xcT[:, b % HB], tiles(XCT_BANK[b])).then_inc(xcT_stored[b], 1)

            def load_table(func):
                act.activation(unread[:], unread_in[:], func)

            def exps(b):
                act.wait_ge(nmax_ready, b + 1)
                for t in range(LT):
                    i = b * LT + t
                    last = act.activation(pexp[:, b, t, :], tiles(E_BANK[b])[:, t, :], ACT.Exp,
                                          bias=nmax[:, i:i + 1], accum_out=psums[:, i:i + 1])
                last.then_inc(exp_ready, 1)

            def store_probT(b):
                act.wait_ge(probT_ready, b + 1)
                part = probT if b == 1 else probT_hi[:, b % HB]
                act.copy(part, tiles(PT_BANK[b])).then_inc(probT_hi_ready, 1)

            def center(b):
                act.wait_ge(nmean_ready, 1)
                for t in range(LT):
                    last = act.activation(xc[:, b * LT + t, :], x_sb[:, b * LT + t, :], ACT.Identity,
                                          bias=nmean[:, t:t + 1])
                last.then_inc(xc_ready[b], 1)

            def scale_xn(b):
                act.wait_ge(x1c_ready, b // HB + 1)
                act.wait_ge(rsqrt_step, rsqrt_steps(2, b // HB, RSQRT_STEPS))
                for i in range(b * LT, (b + 1) * LT):
                    last = act.activation(xn[:, i, :], xn[:, i, :], ACT.Copy, scale=rstd2[:, i:i + 1])
                last.then_inc(xn_ready[0], 1)

            def store_xnT_hi(b):
                act.wait_ge(xnT_ready, turn(b) + 1)
                act.copy(xnT_hi[:, :, b * L:(b + 1) * L], tiles(XNT_BANK[b])).then_inc(xnT_hi_ready, 1)

            def store_x1T(b):
                act.wait_ge(x1T_ready, b + 1)
                act.copy(x1T[:, :, b * L:(b + 1) * L], tiles(X1T_BANK[b])).then_inc(x1T_stored, 1)

            def routing_tanh(h):
                act.wait_ge(margin_ready, h + 1)
                act.activation(tanh_sb[:], margin[:], ACT.Tanh, scale=0.5).then_inc(tanh_ready, 1)

            def store_combT(h):
                act.wait_ge(combT_ready, h + 1)
                act.copy(combT[:], COMBT_BANK[:, :]).then_inc(combT_stored, 1)

            def store_rows(h):
                act.wait_ge(combT_ready, h + 1)
                rows = slice(ROWS, ROWS + E + 1)
                act.copy(comb_rows[rows, h, :], COMBT_BANK[rows, :]).then_inc(rows_stored, 1)

            act.wait_ge(warm_ready, 1)
            load_table(ACT.Exp)
            for i in range(HB):
                store_q(i)
                store_k(i)
            store_xcT(0)
            exps(0)
            store_plain_xcT(0)
            exps(1)
            store_probT(0)
            store_xcT(1)
            store_probT(1)
            store_q(2)
            store_k(2)
            split_hi(0)
            center(3)
            split_hi(1)
            for b in (2, 3):
                store_xcT(b)
                store_plain_xcT(b)
            scale_xn(0)
            store_xnT_hi(1)
            store_xnT_hi(0)
            for b in range(HB, B):
                exps(b)
            load_table(ACT.Silu)
            for g in range(2 * UNITS):
                act.wait_ge(gate_ready, g + 1)
                if g >= 2:
                    act.wait_ge(weighted_ready, g - 1)
                act.activation(silu_sb[:, g % 2, :], gate_ps[:, :], ACT.Silu).then_inc(silu_ready, 1)
                if g == 0:
                    routing_tanh(0)
                    store_x1T(0)
                    store_x1T(1)
                    store_probT(2)
                    store_probT(3)
                    store_combT(0)
                    store_rows(0)
                    split_hi(2)
                    split_hi(3)
                if g >= 2:
                    act.wait_ge(down_ready, g - 1)
                for i, cols in enumerate(columns(g)):
                    act.wait_ge(act_ready, g + 1 + i)
                    act.copy(act_hi[:, g % 2, cols], act_sb[:, cols]).then_inc(act_hi_ready, 1)
                if g == 4:
                    scale_xn(2)
                elif g == 5:
                    store_xnT_hi(3)
                    store_xnT_hi(2)
                    store_x1T(2)
                elif g == 6:
                    store_x1T(3)
                    routing_tanh(1)
                elif g == 8:
                    store_rows(1)
                if SPLIT0 + g < UNITS:
                    split_hi(SPLIT0 + g)

            store_out(act, 1, 1)

        @block.vector
        def _(dve):
            count = [0]

            def then(ins):
                count[0] += 1
                ins.then_inc(dve_step, 1)
                dve.wait_ge(dve_step, count[0])

            def rsqrt(norm, h, first=0, last=RSQRT_STEPS):
                n0, n1 = h * HT, (h + 1) * HT
                var = (mv, mv2)[norm - 1][:, n0:n1, 1]
                y = (rstd, rstd2)[norm - 1][:, n0:n1]
                v, s, t = veps[:, n0:n1], seed[:, n0:n1], yy[:, n0:n1]
                for n in range(first, last):
                    if n == 0:
                        dve.wait_ge((mean_ready, mean2_ready)[norm - 1], (h + 1) * HB)
                    else:
                        dve.wait_ge(rsqrt_step, rsqrt_steps(norm, h, n))
                    a, c = ((-RSQRT_A, RSQRT_A * RSQRT_B), (-0.5, 1.5))[n // 3 == 2]
                    if n == 0:
                        step = dve.tensor_scalar(v, var, EPS, None, ALU.add)
                    elif n == 1:
                        step = dve.tensor_scalar(s, v.bitcast(I32), 1, None, ALU.logical_shift_right)
                    elif n == 2:
                        step = dve.tensor_scalar(y.bitcast(I32), s, -1.0, RSQRT_SEED, ALU.mult, ALU.add)
                    elif n % 3 == 0:
                        step = dve.scalar_tensor_tensor(t, y, a, y, ALU.mult, ALU.mult)
                    elif n % 3 == 1:
                        step = dve.tensor_tensor(t, t, v, ALU.mult)
                    else:
                        step = dve.scalar_tensor_tensor(y, t, c, y, ALU.add, ALU.mult)
                    step.then_inc(rsqrt_step, 1)

            def moments(src, st, m, b):
                for i in range(b * LT, (b + 1) * LT):
                    last = dve.bn_stats(st[:, i, :], src[:, i, :])
                then(last)
                for i in range(b * LT, (b + 1) * LT):
                    last = dve.bn_aggr(m[:, i, :], st[:, i, :])
                return last

            def norm1_moments(b):
                dve.wait_ge(x_in[b], 16)
                moments(x_sb, stats, mv, b).then_inc(mean_ready, 1)

            def norm1_nmean(b):
                dve.wait_ge(mean_ready, b + 1)
                dve.tensor_scalar(nmean[:], mv[:, b * LT:(b + 1) * LT, 0], -1.0, None,
                                  ALU.mult).then_inc(nmean_ready, 1)

            def row_max(b):
                dve.wait_ge(energy_ready, b + 1)
                dve.reduce_max(nmax[:, b * LT:(b + 1) * LT], tiles(E_BANK[b]), AX.X,
                               negate=True).then_inc(nmax_ready, 1)

            def normalise(b):
                dve.wait_ge(exp_ready, b + 1)
                then(dve.reciprocal(rsum[:, b * LT:(b + 1) * LT], psums[:, b * LT:(b + 1) * LT]))
                for t in range(LT):
                    i = b * LT + t
                    last = dve.tensor_scalar(pexp[:, b, t, :], pexp[:, b, t, :], rsum[:, i:i + 1], None, ALU.mult)
                last.then_inc(prob_ready, 1)

            def store_probT_lo(b):
                dve.wait_ge(probT_hi_ready, b + 1)
                dve.tensor_tensor(probT_lo[:, b % HB], tiles(PT_BANK[b]), probT_hi[:, b % HB].bitcast(F32),
                                  ALU.subtract).then_inc(probT_lo_ready, 1)

            def add_attention(b):
                dve.wait_ge(rsqrt_step, rsqrt_steps(1, b // HB, RSQRT_STEPS))
                dve.wait_ge(xm_ready, b + 1)
                for t in range(LT):
                    i = b * LT + t
                    last = dve.scalar_tensor_tensor(x1[:, i, :], tiles(XM_BANK[b])[:, t, :], rstd[:, i:i + 1],
                                                    x_sb[:, i, :], ALU.mult, ALU.add)
                last.then_inc(x1_ready, 1)

            def norm2_moments(b):
                dve.wait_ge(x1_ready, b + 1)
                moments(x1, stats2, mv2, b).then_inc(mean2_ready, 1)

            def norm2(b):
                dve.wait_ge(rsqrt_step, rsqrt_steps(2, b // HB, RSQRT_STEPS))
                for i in range(b * LT, (b + 1) * LT):
                    last = dve.tensor_scalar(xn[:, i, :], x1[:, i, :], mv2[:, i, 0:1], rstd2[:, i:i + 1],
                                             ALU.subtract, ALU.mult)
                last.then_inc(xn_ready[1], 1)

            def store_xnT_lo(b):
                dve.wait_ge(xnT_hi_ready, turn(b) + 1)
                cols = slice(b * L, (b + 1) * L)
                dve.tensor_tensor(xnT_lo[:, :, cols], tiles(XNT_BANK[b]), xnT_hi[:, :, cols].bitcast(F32),
                                  ALU.subtract).then_inc(xnT_lo_ready, 1)

            def top_two(h):
                dve.wait_ge(score_ready, h + 1)
                then(dve.tensor_reduce(score[:], scores_ps.rearrange("p t (i r) -> p t r i", i=2), AX.X, ALU.add))
                for t in range(HT):
                    dve.max(top[:, t, :], score[:, t, 0:E])
                then(dve.tensor_copy(margin[:, :, 1], score[:, :, E]))
                dve.tensor_tensor(margin[:, :, 0], top[:, :, 0], top[:, :, 1],
                                  ALU.subtract).then_inc(margin_ready, 1)
                for t in range(HT):
                    last = dve.max_index(topi[:, t, :], top[:, t, :], score[:, t, 0:E])
                then(last)

            def combine(h):
                comb = comb_parts[:, :, ROWS:ROWS + E + 1].bitcast(F32)
                for i, pick in enumerate((pick0, pick1)):
                    last = dve.tensor_tensor(pick[:], iota8[:], topi[:, :, i:i + 1].broadcast_to([P, HT, E]),
                                             ALU.is_equal)
                then(last)
                then(dve.tensor_tensor(differ[:], pick0[:], pick1[:], ALU.subtract))
                dve.wait_ge(tanh_ready, h + 1)
                then(dve.tensor_scalar(share[:], tanh_sb[:, :, 0], 0.5, 0.5, ALU.mult, ALU.add))
                dve.tensor_scalar(comb[:, :, E], tanh_sb[:, :, 1], 0.5, 0.5, ALU.mult, ALU.add)
                then(dve.tensor_tensor(differ[:], differ[:], share[:].rearrange("p (t i) -> p t i", i=1)
                                       .broadcast_to([P, HT, E]), ALU.mult))
                last = dve.tensor_tensor(comb[:, :, 0:E], differ[:], pick1[:], ALU.add)
                if h == 0:
                    then(last)
                    then(dve.tensor_copy(comb_parts[:, :, 0:E + 1], comb))
                    last = dve.tensor_tensor(comb_parts[:, :, E + 1:2 * (E + 1)], comb,
                                             comb_parts[:, :, 0:E + 1].bitcast(F32), ALU.subtract)
                last.then_inc(comb_ready, 1)

            def finish(h):
                dve.wait_ge(x1T_stored, (h + 1) * HB)
                for k in range(KT):
                    if k == 0:
                        dve.wait_ge(sums_ready, h + 1)
                    else:
                        dve.wait_ge(down_ready, (h + 1) * UNITS)
                    rows = x1T[:, k, h * N:(h + 1) * N]
                    dve.tensor_tensor(rows, acc_ps[k][:, :], rows, ALU.add).then_inc(out_ready, 1)

            dve.memset(unread_in[:], 0.0)
            dve.memset(warm[:], 0.0).then_inc(warm_ready, 1)
            for b in range(B):
                norm1_moments(b)
            norm1_nmean(3)
            row_max(0)
            rsqrt(1, 0, 0, 2)
            row_max(1)
            rsqrt(1, 0, 2, 3)
            normalise(0)
            rsqrt(1, 0, 3, 4)
            normalise(1)
            rsqrt(1, 0, 4, 7)
            store_probT_lo(0)
            rsqrt(1, 0, 7)
            for b in range(HB):
                add_attention(b)
                norm2_moments(b)
            rsqrt(2, 0)
            norm2(1)
            row_max(2)
            store_xnT_lo(1)
            store_xnT_lo(0)
            row_max(3)
            for b in range(HB, B):
                normalise(b)
            dve.wait_ge(const_ready, 1)
            top_two(0)
            combine(0)
            store_probT_lo(2)
            store_probT_lo(3)
            rsqrt(1, 1, 0, 3)
            for g in range(2 * UNITS):
                dve.wait_ge(silu_ready, g + 1)
                if g < SH:
                    dve.wait_ge(cb_ready, 1)
                    weights = comb_ps[:, :]
                else:
                    e = g % UNITS - SH if g % UNITS >= SH else E
                    dve.wait_ge(comb_in[e], 32 if g >= UNITS and e < E else 16)
                    weights = comb_all[:, e, :]
                dve.tensor_tensor(weighted[:], weights, silu_sb[:, g % 2, :], ALU.mult).then_inc(weighted_ready, 1)
                dve.wait_ge(weighted_ready, g + 1)
                dve.wait_ge(up_ready, g + 1)
                for cols in columns(g):
                    dve.tensor_tensor(act_sb[:, cols], UP_BANK[g][:, cols], weighted[:, cols],
                                      ALU.mult).then_inc(act_ready, 1)
                if g == 0:
                    rsqrt(1, 1, 3, 6)
                elif g == 1:
                    add_attention(2)
                elif g == 2:
                    norm2_moments(2)
                elif g == 3:
                    rsqrt(2, 1, 0, 3)
                elif g == 4:
                    norm2(3)
                elif g == 7:
                    combine(1)
                for i, cols in enumerate(columns(g)):
                    dve.wait_ge(act_hi_ready, g + 1 + i)
                    dve.tensor_tensor(act_lo[:, g % 2, cols], act_sb[:, cols], act_hi[:, g % 2, cols].bitcast(F32),
                                      ALU.subtract).then_inc(act_lo_ready, 1)
                if g == 0:
                    rsqrt(1, 1, 6)
                elif g == 1:
                    add_attention(3)
                elif g == 2:
                    norm2_moments(3)
                elif g == 3:
                    rsqrt(2, 1, 3)
                elif g == 5:
                    store_xnT_lo(3)
                    store_xnT_lo(2)
                elif g == 6:
                    top_two(1)
                elif g == UNITS:
                    finish(0)
            finish(1)

        @block.tensor
        def _(pe):
            def project(i):
                c0, c1 = CTX[i]
                pe.wait_ge(proj_in[i], 16)
                for w, ps, stored in ((wqT, Q_BANK[i], q_stored), (wkT, K_BANK[i], k_stored)):
                    if i == HB:
                        pe.wait_ge(stored, 1)
                    pe.matmul(ps[:, 0:c1 - c0], w, ctxT[:, c0:c1], start=True, stop=True).then_inc(qk_ready, 1)

            def transpose4(dst, src):
                for k in range(KT):
                    for t in range(LT):
                        last = pe.transpose(dst[:, k, t * P:(t + 1) * P], src[:, t, k * P:(k + 1) * P], ident[:])
                return last

            def energy(b):
                pe.wait_ge(q_stored, min(b, HB) + 1)
                pe.wait_ge(k_stored, min(b, HB) + 1)
                for t in range(LT):
                    n = b * L + t * P
                    last = pe.matmul(tiles(E_BANK[b])[:, t, :], qT[:, n:n + P], kT[:, b * L:(b + 1) * L],
                                     start=True, stop=True)
                last.then_inc(energy_ready, 1)

            def transpose_xc(b):
                pe.wait_ge(xc_ready[b], 1)
                transpose4(tiles(XCT_BANK[b]), xc[:, b * LT:(b + 1) * LT, :]).then_inc(xcT_ready, 1)

            def transpose_prob(b):
                pe.wait_ge(prob_ready, b + 1)
                transpose4(tiles(PT_BANK[b]), pexp[:, b]).then_inc(probT_ready, 1)

            def attend(b):
                pe.wait_ge(xcT_hi_ready, b + 1)
                pe.wait_ge(probT_hi_ready, b + 1)
                for x_part, p_part in ((xcT_hi, probT_hi), (xcT_lo, probT_hi), (xcT_hi, probT_lo)):
                    if x_part is xcT_lo:
                        pe.wait_ge(xcT_lo_ready[b], 1)
                    elif p_part is probT_lo:
                        pe.wait_ge(probT_lo_ready, max(b, 1))
                    for t in range(LT):
                        for k in range(KT):
                            last = pe.matmul(tiles(XM_BANK[b])[:, t, :], x_part[:, b % HB, k, t * P:(t + 1) * P],
                                             p_part[:, b % HB, k, :], start=(x_part is xcT_hi and p_part is
                                                                             probT_hi and t == 0 and k == 0),
                                             stop=(p_part is probT_lo and t == LT - 1 and k == KT - 1))
                last.then_inc(xm_ready, 1)

            def attend_plain():
                pe.wait_ge(xcT_hi_ready, 2)
                pe.wait_ge(probT_hi_ready, 2)
                for t in range(LT):
                    for k in range(KT):
                        last = pe.matmul(tiles(XM_BANK[1])[:, t, :], xcT[:, 1, k, t * P:(t + 1) * P], probT[:, k, :],
                                         start=(k == 0), stop=(k == KT - 1))
                last.then_inc(xm_ready, 1)

            def warm_up(n):
                for _ in range(n):
                    pe.matmul(warm_ps[:, :], warm[:, 0:P], warm[:], start=True, stop=True)

            def transpose_xn(b):
                pe.wait_ge(xn_ready[b % HB], b // HB + 1)
                transpose4(tiles(XNT_BANK[b]), xn[:, b * LT:(b + 1) * LT, :]).then_inc(xnT_ready, 1)

            def transpose_x1(b):
                pe.wait_ge(x1_ready, b + 1)
                transpose4(tiles(X1T_BANK[b]), x1[:, b * LT:(b + 1) * LT, :]).then_inc(x1T_ready, 1)

            def route(h):
                pe.wait_ge(router_split, 1)
                pe.wait_ge(xcT_stored[3], 1)
                pe.wait_ge(xnT_lo_ready, (h + 1) * HB)
                for t in range(HT):
                    cols = slice(h * N + t * P, h * N + (t + 1) * P)
                    parts = [(a, k) for k in range(KT) for a in (xnT_lo, xnT_hi)]
                    for i, (a, k) in enumerate(parts):
                        last = pe.matmul(scores_ps[:, t, :], a[:, k, cols],
                                         router_parts[:, k].rearrange("p i r -> p (i r)"),
                                         start=(i == 0), stop=(i == len(parts) - 1))
                last.then_inc(score_ready, 1)

            def transpose_comb(h):
                pe.wait_ge(comb_ready, h + 1)
                for t in range(HT):
                    last = pe.transpose(COMBT_BANK[:, t * P:(t + 1) * P], comb_parts[:, t, :].bitcast(F32),
                                        ident[:])
                last.then_inc(combT_ready, 1)

            def weights_of_tokens():
                pe.wait_ge(combT_stored, 1)
                pe.wait_ge(x1T_stored, 2)
                pe.matmul(comb_ps[:, :], select[:], combT[:], start=True, stop=True).then_inc(cb_ready, 1)

            def hidden(g, kind, ps):
                h = g // UNITS
                for i, (w, a, ready) in enumerate(((ffn_hi, xnT_hi, xnT_hi_ready), (ffn_lo, xnT_hi, xnT_hi_ready),
                                                   (ffn_hi, xnT_lo, xnT_lo_ready))):
                    pe.wait_ge(ready, (h + 1) * HB)
                    for k in range(KT):
                        last = pe.matmul(ps[:, :], w_of(w, g, kind, k), a[:, k, h * N:(h + 1) * N],
                                         start=(i == 0 and k == 0), stop=(i == 2 and k == KT - 1))
                return last

            def first_gate():
                for weights, a, ready in (((ffn_hi, ffn_lo), xnT_hi, xnT_hi_ready), ((ffn_hi,), xnT_lo, xnT_lo_ready)):
                    for b in (1, 0):
                        pe.wait_ge(ready, turn(b) + 1)
                        for w in weights:
                            for k in range(KT):
                                last = pe.matmul(tiles(gate_ps)[:, b, :], w_of(w, 0, 0, k),
                                                 a[:, k, b * L:(b + 1) * L],
                                                 start=(w is ffn_hi and a is xnT_hi and b == 1 and k == 0),
                                                 stop=(a is xnT_lo and b == 0 and k == KT - 1))
                return last

            def down(g):
                if g == 0:
                    pe.wait_ge(exp_ready, 3)
                    pe.wait_ge(probT_lo_ready, 2)
                if g == UNITS:
                    pe.wait_ge(out_ready, KT)
                for c, cols in enumerate(columns(g)):
                    pe.wait_ge(act_hi_ready, g + 1 + c)
                    for k in range(KT):
                        for w in (ffn_hi, ffn_lo):
                            pe.matmul(acc_ps[k][:, cols], w_of(w, g, 2, k), act_hi[:, g % 2, cols],
                                      start=(g % UNITS == 0 and w is ffn_hi), stop=False)
                for k in range(KT):
                    for c, cols in enumerate(columns(g)):
                        pe.wait_ge(act_lo_ready, g + 1 + c)
                        last = pe.matmul(acc_ps[k][:, cols], w_of(ffn_hi, g, 2, k), act_lo[:, g % 2, cols],
                                         start=False, stop=(g % UNITS == UNITS - 1 and cols.stop == N))
                    if k == 0 and g % UNITS == UNITS - 1:
                        last.then_inc(sums_ready, 1)
                last.then_inc(down_ready, 1)

            pe.wait_ge(warm_ready, 1)
            warm_up(WARM0)
            project(0)
            project(1)
            energy(0)
            pe.wait_ge(const_ready, 1)
            transpose_xc(0)
            energy(1)
            project(2)
            transpose_prob(0)
            transpose_xc(1)
            transpose_prob(1)
            pe.wait_ge(xcT_stored[0], 1)
            attend(0)
            attend_plain()
            pe.wait_ge(probT_lo_ready, 1)
            transpose_xc(2)
            pe.wait_ge(x1_ready, 1)
            transpose_xc(3)
            energy(2)
            energy(3)
            pe.wait_ge(xcT_stored[2], 1)
            transpose_x1(0)
            transpose_x1(1)
            warm_up(WARM)
            transpose_xn(1)
            transpose_xn(0)

            for g in range(2 * UNITS):
                if g < UNITS:
                    pe.wait_ge(ffn_split, g + 1)
                if g == 1:
                    pe.wait_ge(exp_ready, 4)
                    transpose_prob(2)
                    pe.wait_ge(margin_ready, 1)
                    transpose_prob(3)
                if g >= 1:
                    pe.wait_ge(silu_ready, g)
                (hidden(g, 0, gate_ps) if g else first_gate()).then_inc(gate_ready, 1)
                if g == 0:
                    route(0)
                if g == 1:
                    transpose_comb(0)
                    pe.wait_ge(x1T_stored, 1)
                elif g == 2:
                    pe.wait_ge(act_ready, 1)
                    pe.wait_ge(weighted_ready, SH)
                elif g >= 3:
                    pe.wait_ge(act_ready, g - 1)
                hidden(g, 1, UP_BANK[g]).then_inc(up_ready, 1)
                if g == 1:
                    weights_of_tokens()
                if g == 1:
                    pe.wait_ge(probT_lo_ready, 3)
                    attend(2)
                    pe.wait_ge(rows_stored, 1)
                    attend(3)
                elif g == 5:
                    pe.wait_ge(x1_ready, 3)
                    transpose_xn(3)
                    pe.wait_ge(act_ready, 2)
                    transpose_xn(2)
                    pe.wait_ge(x1_ready, 4)
                    transpose_x1(2)
                elif g == 8:
                    pe.wait_ge(x1T_stored, 3)
                    transpose_comb(1)
                if g >= 1:
                    down(g - 1)
                if g == 6:
                    pe.wait_ge(xnT_lo_ready, turn(2) + 1)
                    transpose_x1(3)
                    route(1)
            down(2 * UNITS - 1)


def kernel(x, ctx_1024, L0_xattn_Wq, L0_xattn_bq, L0_xattn_Wk, L0_xattn_bk, L0_ffn_gate_w, L0_ffn_w_gate,
           L0_ffn_w_up, L0_ffn_w_down, L0_ffn_sh_gate, L0_ffn_sh_up, L0_ffn_sh_down, L0_ffn_se_gate_w):
    import concourse.bacc as bacc
    from concourse.bass_utils import run_bass_kernel_spmd

    def rows(a):
        return np.asarray(a, dtype=np.float32)

    ctxT = rows(ctx_1024).reshape(B * L, D).T
    proj = np.concatenate([rows(L0_xattn_bq)[:, None], rows(L0_xattn_bk)[:, None], rows(L0_xattn_Wq).T,
                           rows(L0_xattn_Wk).T, ctxT], axis=1)
    router = np.concatenate([rows(L0_ffn_gate_w), rows(L0_ffn_se_gate_w), np.zeros((1, L), np.float32)], axis=0)
    router = router.T.reshape(KT, P, R).transpose(1, 0, 2)

    def hidden_blocks(experts, shared):
        w = np.concatenate([rows(shared).reshape(SH, P, L), rows(experts)], axis=0)
        return w.reshape(UNITS, P, KT, P).transpose(0, 3, 2, 1).reshape(UNITS, P, KT * P)

    down = np.concatenate([rows(L0_ffn_sh_down).reshape(L, SH, P).transpose(1, 0, 2), rows(L0_ffn_w_down)], axis=0)
    ffn = np.concatenate([hidden_blocks(L0_ffn_w_gate, L0_ffn_sh_gate), hidden_blocks(L0_ffn_w_up, L0_ffn_sh_up),
                          down.transpose(0, 2, 1)], axis=2)

    nc = bacc.Bacc("TRN2", target_bir_lowering=False, num_devices=1)
    arrays = {"proj": proj, "x": rows(x).reshape(B * LT, P, L), "router": router, "ffn": ffn}
    arrays = {name: np.ascontiguousarray(a) for name, a in arrays.items()}
    args = [nc.dram_tensor(name, a.shape, F32, kind="ExternalInput").ap() for name, a in arrays.items()]
    out = nc.dram_tensor("out", (KT, P, B * L), F32, kind="ExternalOutput").ap()
    comb_dram = nc.dram_tensor("comb_dram", (2, E + 1, N), F32, kind="Internal").ap()
    xattn_moe_kernel(nc, *args, comb_dram, out)
    result = run_bass_kernel_spmd(nc, [arrays], core_ids=[0]).results[0]["out"]
    return np.ascontiguousarray(result.reshape(L, B, L).transpose(1, 2, 0))
```
